# Optimizing a Trainium2 kernel written in Bass

```python
import numpy as np
import jax
import jax.numpy as jnp

def _softmax(x, axis=-1):
    return jax.nn.softmax(x, axis=axis)

def _gelu(x):
    return jax.nn.gelu(x, approximate=True)

def _silu(x):
    return jax.nn.silu(x)

def _sigmoid(x):
    return jax.nn.sigmoid(x)

def _layernorm(x, axis=-1, eps=1e-05):
    m = jnp.mean(x, axis=axis, keepdims=True)
    v = jnp.var(x, axis=axis, keepdims=True)
    return (x - m) / jnp.sqrt(v + eps)

def _scatter_add(tgt, idx, src, axis=0):
    return tgt.at[idx].add(src)

def _segment_sum(src, seg, n):
    return jax.ops.segment_sum(src, seg, n)
kernel_name = 'mk_adaln_d1_jaxref_r8_1cfd9a'

def setup_inputs(seed: int=0):
    np.random.seed(seed)
    _w = jnp.asarray

    def _L0_attn_setup():
        import jax, jax.numpy as jnp
        import numpy as np
        import math
        D_MODEL = 128
        NUM_HEADS = 16
        D_K = D_MODEL // NUM_HEADS
        B, S = (2, 256)

        def _linear_weight(key, out_f, in_f):
            return jax.random.normal(key, (out_f, in_f), jnp.float32) * math.sqrt(2.0 / in_f)
        key = jax.random.key(seed)
        ks = jax.random.split(key, 5)
        x = jax.random.normal(ks[0], (B, S, D_MODEL), jnp.float32)
        return {'x': x, 'Wq': _linear_weight(ks[1], D_MODEL, D_MODEL), 'bq': jnp.zeros((D_MODEL,), jnp.float32), 'Wk': _linear_weight(ks[2], D_MODEL, D_MODEL), 'bk': jnp.zeros((D_MODEL,), jnp.float32), 'Wv': _linear_weight(ks[3], D_MODEL, D_MODEL), 'bv': jnp.zeros((D_MODEL,), jnp.float32), 'Wo': _linear_weight(ks[4], D_MODEL, D_MODEL), 'bo': jnp.zeros((D_MODEL,), jnp.float32)}
    _L0_attn_in = _L0_attn_setup()

    def _L0_ffn_setup():
        import jax, jax.numpy as jnp
        import numpy as np
        TOP_K = 2
        key = jax.random.key(seed)
        ks = jax.random.split(key, 8)
        B, S, D, E = (4, 256, 128, 8)
        H = 4 * D
        x = jax.random.normal(ks[0], (B, S, D), dtype=jnp.float32)
        W1 = jax.random.normal(ks[1], (E, D, H), dtype=jnp.float32) * np.sqrt(2.0 / (D + H))
        b1 = jax.random.normal(ks[2], (E, H), dtype=jnp.float32) * 1e-06
        W2 = jax.random.normal(ks[3], (E, H, D), dtype=jnp.float32) * np.sqrt(2.0 / (H + D))
        b2 = jax.random.normal(ks[4], (E, D), dtype=jnp.float32) * 1e-06
        gate_w = jax.random.normal(ks[5], (D, E), dtype=jnp.float32) * np.sqrt(1.0 / D)
        gate_b = jnp.zeros((E,), dtype=jnp.float32)
        temperature = jnp.asarray(1.0, dtype=jnp.float32)
        return {'x': x, 'W1': W1, 'b1': b1, 'W2': W2, 'b2': b2, 'gate_w': gate_w, 'gate_b': gate_b, 'temperature': temperature}
    _L0_ffn_in = _L0_ffn_setup()
    _L0_c = _w((lambda *s: np.random.randn(*s).astype(np.float32) * 0.05)(4, 128))
    _L0_wmod = _w((lambda *s: np.random.randn(*s).astype(np.float32) * 0.05)(128, 6 * 128) * 128 ** (-0.5))
    _d = {'L0_attn_x': _L0_attn_in['x'], 'L0_attn_Wq': _L0_attn_in['Wq'], 'L0_attn_bq': _L0_attn_in['bq'], 'L0_attn_Wk': _L0_attn_in['Wk'], 'L0_attn_bk': _L0_attn_in['bk'], 'L0_attn_Wv': _L0_attn_in['Wv'], 'L0_attn_bv': _L0_attn_in['bv'], 'L0_attn_Wo': _L0_attn_in['Wo'], 'L0_attn_bo': _L0_attn_in['bo'], 'L0_ffn_W1': _L0_ffn_in['W1'], 'L0_ffn_b1': _L0_ffn_in['b1'], 'L0_ffn_W2': _L0_ffn_in['W2'], 'L0_ffn_b2': _L0_ffn_in['b2'], 'L0_ffn_gate_w': _L0_ffn_in['gate_w'], 'L0_ffn_gate_b': _L0_ffn_in['gate_b'], 'L0_ffn_temperature': _L0_ffn_in['temperature'], 'L0_c': _L0_c, 'L0_wmod': _L0_wmod}
    _x0 = _d['L0_attn_x']
    _d['L0_attn_x'] = jax.random.normal(jax.random.fold_in(jax.random.key(seed), 1), (4, 1024, 128), dtype=_x0.dtype)
    del _x0
    return _d

def reference(L0_attn_x, L0_attn_Wq, L0_attn_bq, L0_attn_Wk, L0_attn_bk, L0_attn_Wv, L0_attn_bv, L0_attn_Wo, L0_attn_bo, L0_ffn_W1, L0_ffn_b1, L0_ffn_W2, L0_ffn_b2, L0_ffn_gate_w, L0_ffn_gate_b, L0_ffn_temperature, L0_c, L0_wmod):

    def _L0_attn_ref(x, Wq, bq, Wk, bk, Wv, bv, Wo, bo):
        import jax, jax.numpy as jnp
        import numpy as np
        import math
        D_MODEL = 128
        NUM_HEADS = 16
        D_K = D_MODEL // NUM_HEADS
        B, S = (2, 256)

        def _linear_weight(key, out_f, in_f):
            return jax.random.normal(key, (out_f, in_f), jnp.float32) * math.sqrt(2.0 / in_f)
        b, s, _ = x.shape
        q = jnp.einsum('bsd,ed->bse', x, Wq) + bq
        k = jnp.einsum('bsd,ed->bse', x, Wk) + bk
        v = jnp.einsum('bsd,ed->bse', x, Wv) + bv
        q = q.reshape(b, s, NUM_HEADS, D_K).transpose(0, 2, 1, 3)
        k = k.reshape(b, s, NUM_HEADS, D_K).transpose(0, 2, 1, 3)
        v = v.reshape(b, s, NUM_HEADS, D_K).transpose(0, 2, 1, 3)
        scores = jnp.einsum('bhqd,bhkd->bhqk', q, k) / math.sqrt(D_K)
        attn = jax.nn.softmax(scores, axis=-1)
        out = jnp.einsum('bhqk,bhkd->bhqd', attn, v)
        out = out.transpose(0, 2, 1, 3).reshape(b, s, D_MODEL)
        return jnp.einsum('bsd,ed->bse', out, Wo) + bo

    def _L0_ffn_ref(x, W1, b1, W2, b2, gate_w, gate_b, temperature):
        import jax, jax.numpy as jnp
        import numpy as np
        TOP_K = 2
        gates = (jnp.einsum('bsd,de->bse', x, gate_w) + gate_b) / temperature
        weights, indices = jax.lax.top_k(gates, TOP_K)
        weights = jax.nn.softmax(weights, axis=-1)
        h = jnp.einsum('bsd,edf->bsef', x, W1) + b1
        h = jax.nn.gelu(h, approximate=False)
        all_out = jnp.einsum('bsef,efd->bsed', h, W2) + b2
        expert_out = jnp.take_along_axis(all_out, indices[..., None], axis=2)
        out = jnp.sum(expert_out * weights[..., None], axis=2)
        return out
    x = L0_attn_x
    mod = (_silu(L0_c) @ L0_wmod).reshape(L0_c.shape[0], 6, 1, -1)
    sa, ca, ga, sb, cb, gb = (mod[:, 0], mod[:, 1], mod[:, 2], mod[:, 3], mod[:, 4], mod[:, 5])
    ga = (2 * (ga >= 0) - 1) * jnp.maximum(jnp.abs(ga), 0.25)
    gb = (2 * (gb >= 0) - 1) * jnp.maximum(jnp.abs(gb), 0.25)
    h = _layernorm(x, axis=-1) * (1 + ca) + sa
    x = x + ga * _L0_attn_ref(h, L0_attn_Wq, L0_attn_bq, L0_attn_Wk, L0_attn_bk, L0_attn_Wv, L0_attn_bv, L0_attn_Wo, L0_attn_bo)
    h = _layernorm(x, axis=-1) * (1 + cb) + sb
    x = x + gb * _L0_ffn_ref(h, L0_ffn_W1, L0_ffn_b1, L0_ffn_W2, L0_ffn_b2, L0_ffn_gate_w, L0_ffn_gate_b, L0_ffn_temperature)
    return x

_drawn_inputs = setup_inputs


def setup_inputs(seed=0):
    import zlib

    import numpy as np

    out = dict(_drawn_inputs(seed))
    spreads = {'L0_attn_bq': (0.0, 0.635),
     'L0_attn_bk': (0.0, 0.8),
     'L0_attn_bv': (0.0, 0.1),
     'L0_attn_bo': (0.0, 0.287),
     'L0_ffn_gate_b': (0.0, 0.336)}
    factors = {'L0_ffn_b1': 8.0, 'L0_ffn_b2': 8.0}
    for name, (base, spread) in spreads.items():
        noise = np.random.default_rng([zlib.crc32(name.encode()), seed]).standard_normal(out[name].shape)
        drawn = base * np.exp(spread * noise) if base else spread * noise
        out[name] = jnp.asarray(drawn.astype(out[name].dtype))
    for name, factor in factors.items():
        out[name] = (out[name] * factor).astype(out[name].dtype)
    return out
```

```python
from contextlib import ExitStack

import concourse.bass as bass
import numpy as np
from concourse import mybir


def adaln_block(nc, x_d, wq_d, bq_d, wk_d, bk_d, wv_d, bv_d, wo_d, bo_d,
                w1_d, b1_d, w2_d, b2_d, gw_d, gb_d, temp_d, c_d, wmod_d, out_d):
    F32, BF16, U32 = mybir.dt.float32, mybir.dt.bfloat16, mybir.dt.uint32
    ALU, ACT, AX = mybir.AluOpType, mybir.ActivationFunctionType, mybir.AxisListType
    ds = bass.ds

    P = 128
    B, S, D = x_d.shape
    E, _, F = w1_d.shape
    H, DK = 16, D // 16
    MOD = 6
    G = 512
    GT = G // P
    KG = S // G
    NG = B * KG
    QT = S // P
    FC = F // P
    SLOTS = 8
    ITERS = B * H // SLOTS
    QUAD = 4
    NPART = 3
    PAIRS = 6
    ROWS = PAIRS * DK
    SHIFT = 2 * ROWS
    KROWS = SHIFT + NPART
    RING = 4
    PV, MISC = 6, 7
    W_LOADS = 13
    SCALE = 1.0 / float(np.sqrt(DK))
    EPS = 1e-5

    ctx = ExitStack()
    with ctx:
        def sb(name, shape, dt=F32):
            return ctx.enter_context(nc.sbuf_tensor(name, shape, dt))

        def sem(name):
            return ctx.enter_context(nc.semaphore(name))

        x_sb = sb("x_sb", [P, NG, GT, D])
        v_all = sb("v_all", [P, B * H * QT * DK])
        o_all = sb("o_all", [P, ITERS * QT * SLOTS * DK])
        q_stack = sb("q_stack", [P, SLOTS, S], BF16)
        k_stack = sb("k_stack", [P, SLOTS // 2, S], BF16)
        v_stage = sb("v_stage", [P, SLOTS, QT, 32])
        probs = sb("probs", [P, RING, S])
        h2T_all = q_stack[:, :, :].rearrange("p a b -> p (a b)").bitcast(F32)
        hid = probs[:, :, :].rearrange("p r (c t) -> p (r c) t", t=G)
        w1 = sb("w1", [P, E, F])
        w2 = sb("w2", [P, E * FC, D])
        wmod = sb("wmod", [P, MOD * D])
        wT = sb("wT", [P, 4, D])
        w_raw = sb("w_raw", [P, 4, D])
        ident = sb("ident", [P, P])
        ident_b = sb("ident_b", [P, P], BF16)
        cT = sb("cT", [P, B])
        silu_t = sb("silu_t", [P, 2, B])
        siluT = sb("siluT", [P, B])
        silu_b = sb("silu_b", [P, B, P])
        mod_c = sb("mod_c", [P, MOD, B])
        gaB = sb("gaB", [P, B, D])
        gbB = sb("gbB", [P, B, D])
        gate_t = sb("gate_t", [P, 2, B, D])
        gaboB = sb("gaboB", [P, B, D])
        boB = sb("boB", [P, D])
        bvB = sb("bvB", [P, D])
        gbiasB = sb("gbiasB", [P, E])
        tempB = sb("tempB", [P, 1])
        rtemp = sb("rtemp", [P, 1])
        b2B = sb("b2B", [P, E, D])
        b1_raw = sb("b1_raw", [E * FC, P])
        b1c = sb("b1c", [P, E * FC])
        bq = sb("bq", [P, 1])
        bk = sb("bk", [P, 1])
        gate_w = sb("gate_w", [P, E])
        mhalf = sb("mhalf", [P, GT])
        stats = sb("stats", [P, KG, GT, 6])
        mv = sb("mv", [P, KG, GT, 2])
        vareps = sb("vareps", [P, KG, GT])
        rstd = sb("rstd", [P, KG, GT])
        xn = sb("xn", [P, KG, GT, D])
        hT = sb("hT", [P, KG, G])
        qf = sb("qf", [P, KG, G])
        kf = sb("kf", [P, KG, G])
        q_parts = sb("q_parts", [P, KG, NPART, G], BF16)
        k_parts = sb("k_parts", [P, KG, NPART, G], BF16)
        nmax = sb("nmax", [P, SLOTS, QT])
        nmax_r = sb("nmax_r", [P, SLOTS, 2, QT])
        nmax_p = sb("nmax_p", [P, SLOTS, NPART, QT], BF16)
        nmaxT = sb("nmaxT", [NPART * QT, SLOTS, P], BF16)
        pv_sb = sb("pv_sb", [P, 2, 2 * P])
        rsum = sb("rsum", [P, 2, 2, 4])
        o_st = qf
        oT = kf
        y_sb = xn
        logits = sb("logits", [P, KG, GT, E])
        eight_v = sb("eight_v", [P, KG, GT, 8])
        eight_i = sb("eight_i", [P, KG, GT, 8], U32)
        top_v = sb("top_v", [P, 2, NG * GT])
        top_if = sb("top_if", [P, 2, NG * GT])
        wts = sb("wts", [P, 4, NG * GT])
        iota_e = sb("iota_e", [P, E])
        hot = sb("hot", [P, 2, NG * GT, E])
        w_exp = sb("w_exp", [P, NG * GT, E])
        acc = sb("acc", [P, 2, GT, D])

        psum = ctx.enter_context(nc.psum_tensor("psum", [P, 8 * 512], F32))

        def bank(n, k=1):
            return psum[:, n * 512:(n + k) * 512]

        q_dram = nc.dram_tensor("q_dram", (B * H, NPART, DK, S), BF16, kind="Internal").ap()
        k_dram = nc.dram_tensor("k_dram", (B * H, NPART, DK, S), BF16, kind="Internal").ap()

        x_loaded, small_loaded, w_loaded, ffn_loaded = sem("x_loaded"), sem("small_loaded"), sem("w_loaded"), sem("ffn_loaded")
        consts_made, ident_made, stacks_cleared = sem("consts_made"), sem("ident_made"), sem("stacks_cleared")
        pool_chain, dve_chain = sem("pool_chain"), sem("dve_chain")
        c_exp_done, silu_done, mod_done, mod_ready, w_transposed, wT_ready = (
            sem(n) for n in ("c_exp_done", "silu_done", "mod_done", "mod_ready", "w_transposed", "wT_ready"))
        mv_ready, rstd_ready, xn_ready, xT_ready, hT_ready = (
            sem(n) for n in ("mv_ready", "rstd_ready", "xn_ready", "xT_ready", "hT_ready"))
        q_mm, k_mm, v_mm, q_evac, k_evac, v_evac, q_split, k_split = (
            sem(n) for n in ("q_mm", "k_mm", "v_mm", "q_evac", "k_evac", "v_evac", "q_split", "k_split"))
        q_written = [sem(f"q_written{k}") for k in range(KG)]
        k_written = [sem(f"k_written{k}") for k in range(KG)]
        q_loaded = [sem(f"q_loaded{s}") for s in range(SLOTS)]
        k_loaded = [sem(f"k_loaded{s}") for s in range(SLOTS // 2)]
        shift_loaded = [sem(f"shift_loaded{s}") for s in range(SLOTS)]
        st_ready, exp_done, mx_ready, mx_free, split_chain, nmax_split, nmaxT_ready, nmaxT_evac = (
            sem(n) for n in ("st_ready", "exp_done", "mx_ready", "mx_free", "split_chain", "nmax_split", "nmaxT_ready", "nmaxT_evac"))
        pv_done, pv_evac, oT_ready, rsum_ready, o_done, v_staged = (
            sem(n) for n in ("pv_done", "pv_evac", "oT_ready", "rsum_ready", "o_done", "v_staged"))
        o_staged, xg_ready, ao_ready, ao_evac, y_mm, y_scaled, x2_ready = (
            sem(n) for n in ("o_staged", "xg_ready", "ao_ready", "ao_evac", "y_mm", "y_scaled", "x2_ready"))
        mv2_ready, rstd2_ready, xn2_ready, x2T_ready, h2_ready, h2_kept, g_mm, g_evac = (
            sem(n) for n in ("mv2_ready", "rstd2_ready", "xn2_ready", "x2T_ready", "h2_ready", "h2_kept", "g_mm", "g_evac"))
        g_chain, w_chain, e_exp, wexp_ready = sem("g_chain"), sem("w_chain"), sem("e_exp"), sem("wexp_ready")
        h_mm, gelu_done, y2_mm, y2_evac, acc_chain, out_ready = (
            sem(n) for n in ("h_mm", "gelu_done", "y2_mm", "y2_evac", "acc_chain", "out_ready"))
        out_stored = [sem(f"out_stored{k}") for k in range(KG)]
        var_chain, var2_chain, st_chain, st2_chain, qs_chain, sm_chain, fin_chain, topi_done = (
            sem(n) for n in ("var_chain", "var2_chain", "st_chain", "st2_chain", "qs_chain", "sm_chain", "fin_chain",
                             "topi_done"))

        waits_apart = sem("waits_apart")

        def wait_apart(eng, semaphore, value):
            eng.wait_ge(semaphore, value)
            eng.sem_inc(waits_apart, 1)

        block = ctx.enter_context(nc.Block())
        x_v = x_d.rearrange("b s d -> (b s) d").rearrange("(g p t) d -> g p t d", p=P, t=GT)
        out_v = out_d.rearrange("b s d -> (b s) d").rearrange("(g p t) d -> g p t d", p=P, t=GT)

        @block.sync
        def _(sp):
            for k in range(KG):
                sp.sem_inc(q_written[k], NPART * 16)
                sp.sem_inc(k_written[k], NPART * 16)
                sp.sem_inc(out_stored[k], 16)
            sp.dma_start(cT[:, :], c_d.rearrange("b d -> d b"), allow_slow_non_contiguous=True).then_inc(small_loaded, 16)
            sp.dma_start(wmod[:, :], wmod_d).then_inc(small_loaded, 16)
            sp.dma_start(x_sb[:, :, :, :], x_v.rearrange("g p t d -> p g (t d)")).then_inc(x_loaded, 16)
            for n, w in enumerate((wq_d, wk_d, wv_d, wo_d)):
                sp.dma_start(w_raw[:, n, :], w).then_inc(w_loaded, 16)
            for dst, src in ((bq, bq_d), (bk, bk_d)):
                sp.dma_start(dst[:, :], src.rearrange("(d a) -> d a", a=1), allow_slow_non_contiguous=True).then_inc(w_loaded, 16)
            for dst, src in ((bvB[:, :], bv_d), (boB[:, :], bo_d), (gbiasB[:, :], gb_d)):
                sp.dma_start(dst, src.partition_broadcast(P)).then_inc(w_loaded, 16)
            sp.dma_start(tempB[:, :], temp_d.partition_broadcast(P)).then_inc(w_loaded, 16)
            sp.dma_start(gate_w[:, :], gw_d).then_inc(w_loaded, 16)
            sp.dma_start(b1_raw[:, :], b1_d.rearrange("e (c f) -> (e c) f", f=P)).then_inc(w_loaded, 16)
            sp.dma_start(b2B[:, :, :].rearrange("p e d -> p (e d)"),
                         b2_d.rearrange("e d -> (e d)").partition_broadcast(P)).then_inc(w_loaded, 16)
            with sp.Fori(0, B) as b:
                for k in range(KG):
                    for split, parts, dram, written in ((q_split, q_parts, q_dram, q_written),
                                                        (k_split, k_parts, k_dram, k_written)):
                        sp.wait_ge(split, 2 + b * KG + k + 1)
                        for n in range(NPART):
                            sp.dma_start(dram[ds(b * H, H), n, :, k * G:(k + 1) * G],
                                         parts[:, k, n, :]).then_inc(written[k], 16)
            sp.dma_start(w1[:, :, :], w1_d.rearrange("e d f -> d e f")).then_inc(ffn_loaded, 16)
            sp.dma_start(w2[:, :, :], w2_d.rearrange("e (c f) d -> f (e c) d", f=P)).then_inc(ffn_loaded, 16)

            for k in range(KG):
                sp.wait_ge(q_written[k], (B + 1) * NPART * 16)
                sp.wait_ge(k_written[k], (B + 1) * NPART * 16)

            def load_q(i, s):
                r = (s % 2) * ROWS
                for n, at in ((3, 0), (2, 3), (1, 5)):
                    src = q_dram[ds(i * SLOTS + s, 1), 0:n, :, :].rearrange("a n d t -> (a n d) t")
                    sp.dma_start(q_stack[r + at * DK:r + (at + n) * DK, s, :], src).then_inc(q_loaded[s], 16)

            def load_k(i, s):
                r = (s % 2) * ROWS
                at = 0
                for part, n in ((0, 3), (1, 2), (2, 1)):
                    for _ in range(n):
                        src = k_dram[ds(i * SLOTS + s, 1), part:part + 1, :, :].rearrange("a n d t -> (a n d) t")
                        sp.dma_start(k_stack[r + at * DK:r + (at + 1) * DK, s // 2, :], src)\
                          .then_inc(k_loaded[s // 2], 16)
                        at += 1

            def store_shift(m_count, s):
                sp.wait_ge(nmaxT_evac, 1 + m_count)
                sp.dma_start(q_stack[SHIFT:KROWS, s, :], nmaxT[:, s, :]).then_inc(shift_loaded[s], 16)

            sp.wait_ge(stacks_cleared, 3)
            for s in range(SLOTS):
                load_q(0, s)
                load_k(0, s)
            for s in range(QUAD - 1):
                store_shift(s + 1, s)

            def attention(i, last):
                for s in range(SLOTS):
                    if not last or s <= QUAD:
                        store_shift(SLOTS * i + s + QUAD, (s + QUAD - 1) % SLOTS)
                    if not last:
                        sp.wait_ge(st_ready, SLOTS * 16 * i + 16 * (s + 1))
                        load_q(i + 1, s)
                        if s % 2:
                            load_k(i + 1, s - 1)
                            load_k(i + 1, s)

            with sp.Fori(0, ITERS - 1) as i:
                attention(i, False)
            attention(ITERS - 1, True)

            with sp.Fori(0, B) as b:
                for k in range(KG):
                    sp.wait_ge(out_ready, b * KG + k + 1)
                    sp.dma_start(out_v[ds(b * KG + k, 1), :, :, :].rearrange("g p t d -> (g p) (t d)"),
                                 acc[:, k, :, :].rearrange("p t d -> p (t d)")).then_inc(out_stored[k], 16)
            for k in range(KG):
                sp.wait_ge(out_stored[k], (B + 1) * 16)

        @block.gpsimd
        def _(pool):
            pool.sem_inc(h2_kept, KG)
            chain = [0]

            def link(ins):
                chain[0] += 1
                ins.then_inc(pool_chain, 1)
                pool.wait_ge(pool_chain, chain[0])

            link(nc.gpsimd.memset(ident[:, :], 0.0))
            link(nc.gpsimd.memset(ident_b[:, :], 0.0))
            for m in (ident, ident_b):
                nc.gpsimd.affine_select(out=m[:, :], in_=m[:, :], compare_op=ALU.not_equal, fill=1.0,
                                        base=0, pattern=[[-1, P]], channel_multiplier=1).then_inc(ident_made, 1)
            pool.wait_ge(ident_made, 2)
            nc.gpsimd.memset(mhalf[:, :], -0.5).then_inc(consts_made, 1)
            pool.wait_ge(consts_made, 1)
            for n, (part, value) in enumerate(((q_stack[:, :, :], 0.0), (k_stack[SHIFT:P, :, :], 1.0),
                                               (v_stage[:, :, :, :], 0.0))):
                nc.gpsimd.memset(part, value).then_inc(stacks_cleared, 1)
                pool.wait_ge(stacks_cleared, n + 1)
            for s in range(SLOTS):
                last = nc.gpsimd.memset(v_stage[:, s, :, DK:DK + 1], 1.0)
            link(last)

            def rstd_of(k, count, ready, done, v_chain):
                wait_apart(pool, ready, count)
                nc.gpsimd.tensor_scalar(vareps[:, k, :], mv[:, k, :, 1], EPS, None, ALU.add).then_inc(v_chain, 1)
                pool.wait_ge(v_chain, count)
                nc.gpsimd.tensor_tensor(rstd[:, k, :], vareps[:, k, :], mhalf[:, :], ALU.pow).then_inc(done, 1)

            ks_chain = split_chain
            with pool.Fori(0, B) as b:
                for k in range(KG):
                    g = b * KG + k
                    rstd_of(k, g + 1, mv_ready, rstd_ready, var_chain)
                    wait_apart(pool, k_evac, 2 + g + 1)
                    wait_apart(pool, k_written[k], (b + 1) * NPART * 16)
                    part = [k_parts[:, k, n, :] for n in range(NPART)]
                    nc.gpsimd.tensor_copy(part[0], kf[:, k, :]).then_inc(ks_chain, 1)
                    wait_apart(pool, ks_chain, g * 3 + 1)
                    nc.gpsimd.tensor_tensor(kf[:, k, :], kf[:, k, :], part[0], ALU.subtract).then_inc(ks_chain, 1)
                    wait_apart(pool, ks_chain, g * 3 + 2)
                    nc.gpsimd.tensor_copy(part[1], kf[:, k, :]).then_inc(ks_chain, 1)
                    wait_apart(pool, ks_chain, g * 3 + 3)
                    nc.gpsimd.tensor_tensor(part[2], kf[:, k, :], part[1], ALU.subtract).then_inc(k_split, 1)

            def stage_v(i, quad, pv_count):
                wait_apart(pool, pv_done, pv_count)
                W = QUAD * QT * DK
                nc.gpsimd.tensor_copy(
                    v_stage[:, quad * QUAD:(quad + 1) * QUAD, :, 0:DK].rearrange("p s k d -> p (s k) d"),
                    v_all[:, ds(i * 2 * W + quad * W, W)].rearrange("p (s d) -> p s d", d=DK)).then_inc(v_staged, 1)

            def split_max(m, s):
                wait_apart(pool, mx_free, 2 + QT * (m + 1))
                r1, r2 = nmax_r[:, s, 0, :], nmax_r[:, s, 1, :]
                part = [nmax_p[:, s, n, :] for n in range(NPART)]
                nc.gpsimd.tensor_copy(part[0], nmax[:, s, :]).then_inc(sm_chain, 1)
                wait_apart(pool, sm_chain, 4 * m + 1)
                nc.gpsimd.tensor_tensor(r1, nmax[:, s, :], part[0], ALU.subtract).then_inc(sm_chain, 1)
                wait_apart(pool, sm_chain, 4 * m + 2)
                nc.gpsimd.tensor_copy(part[1], r1).then_inc(sm_chain, 1)
                wait_apart(pool, sm_chain, 4 * m + 3)
                nc.gpsimd.tensor_tensor(r2, r1, part[1], ALU.subtract).then_inc(sm_chain, 1)
                wait_apart(pool, sm_chain, 4 * m + 4)
                nc.gpsimd.tensor_copy(part[2], r2).then_inc(nmax_split, 1)

            pool.wait_ge(v_evac, 2 + NG)
            stage_v(0, 0, RING)
            for m in range(QUAD):
                split_max(m, m)

            def attention(i, last):
                for s in range(SLOTS):
                    if s == 0:
                        stage_v(i, 1, RING + QT * SLOTS * i)
                    if not last or s < QUAD:
                        split_max(SLOTS * i + s + QUAD, (s + QUAD) % SLOTS)
                    if s == QUAD and not last:
                        stage_v(i + 1, 0, RING + QT * (SLOTS * i + QUAD))

            with pool.Fori(0, ITERS - 1) as i:
                attention(i, False)
            attention(ITERS - 1, True)

            IW = QT * SLOTS * DK
            pool.wait_ge(o_done, 1 + B * H)
            with pool.Fori(0, B) as b:
                for k in range(KG):
                    g = b * KG + k
                    wait_apart(pool, ao_ready, (b + 1) * KG)
                    o_v = o_all[:, ds(b * 2 * IW, 2 * IW)].rearrange("p (a t e) -> p t a e", a=2, t=QT)
                    for t in range(GT):
                        last = nc.gpsimd.tensor_copy(
                            o_st[:, k, t * D:(t + 1) * D].rearrange("p (a e) -> p a e", a=2),
                            o_v[:, k * GT + t, :, :])
                    last.then_inc(o_staged, 1)
                    for t in range(GT):
                        xt = x_sb[:, ds(g, 1), t, :].rearrange("p a d -> p (a d)")
                        last = nc.gpsimd.tensor_tensor(
                            xt, xt, gaboB[:, ds(b, 1), :].rearrange("p a d -> p (a d)"), ALU.add)
                    last.then_inc(xg_ready, 1)
                    rstd_of(k, g + 1, mv2_ready, rstd2_ready, var2_chain)
                    wait_apart(pool, h2_ready, 2 + g + 1)
                    nc.gpsimd.tensor_copy(h2T_all[:, ds(g * G, G)], hT[:, k, :]).then_inc(h2_kept, 1)

        @block.scalar
        def _(act):
            act.sem_inc(hT_ready, 2)
            act.sem_inc(q_evac, 2)
            act.sem_inc(k_evac, 2)
            act.sem_inc(exp_done, 2)
            act.sem_inc(pv_evac, 1)
            act.sem_inc(nmaxT_evac, 1)
            act.sem_inc(h2_ready, 2)
            act.sem_inc(ao_evac, 2)
            act.sem_inc(gelu_done, 4)
            act.wait_ge(small_loaded, 32)
            nc.scalar.activation(silu_t[:, 0, :], cT[:, :], ACT.Exp, scale=-1.0).then_inc(c_exp_done, 1)
            act.wait_ge(w_transposed, 1)
            nc.scalar.activation(wT[:, :, :].rearrange("p a b -> p (a b)"), bank(0), ACT.Copy).then_inc(wT_ready, 1)
            nc.scalar.activation(b1c[:, :], bank(1)[:, 0:E * FC], ACT.Copy).then_inc(wT_ready, 1)
            act.wait_ge(mod_ready, 1)
            act.wait_ge(w_loaded, W_LOADS * 16)
            with act.Fori(0, B) as b:
                for k in range(KG):
                    g = b * KG + k
                    wait_apart(act, xT_ready, g + 1)
                    nc.scalar.activation(hT[:, k, :], bank(k), ACT.Identity,
                                         bias=mod_c[:, 0, ds(b, 1)], scale=mod_c[:, 1, ds(b, 1)]).then_inc(hT_ready, 1)
                    act.wait_ge(q_mm, g + 1)
                    act.wait_ge(q_split, g + 1)
                    nc.scalar.activation(qf[:, k, :], bank(2 + k), ACT.Identity, bias=bq[:, :]).then_inc(q_evac, 1)
                    act.wait_ge(k_mm, g + 1)
                    act.wait_ge(k_split, g + 1)
                    nc.scalar.activation(kf[:, k, :], bank(4 + k), ACT.Identity, bias=bk[:, :]).then_inc(k_evac, 1)

            def evac_shift(m, s):
                act.wait_ge(nmaxT_ready, m + 1)
                nc.scalar.activation(nmaxT[:, s, :], bank(MISC)[0:NPART * QT, 0:P // 2].bitcast(BF16),
                                     ACT.Copy).then_inc(nmaxT_evac, 1)

            def evac_pv(n, s):
                act.wait_ge(pv_done, RING + QT * (n + 1))
                nc.scalar.activation(pv_sb[:, s % 2, :], bank(PV)[:, 0:2 * P], ACT.Copy).then_inc(pv_evac, 1)

            for m in range(QUAD - 1):
                evac_shift(m, m)

            def attention(i, last):
                for s in range(SLOTS):
                    n = SLOTS * i + s
                    for kt in range(QT):
                        act.wait_ge(pv_done, QT * n + kt + 1)
                        for half in range(2):
                            act.wait_ge(st_ready, 16 * n + 2 * kt + half + 1)
                            nc.scalar.activation(probs[:, kt % RING, half * 512:(half + 1) * 512], bank(half),
                                                 ACT.Exp, scale=SCALE).then_inc(exp_done, 1)
                        if kt == 0 and s:
                            evac_pv(n - 1, s - 1)
                        if kt == 5 and (not last or s <= QUAD):
                            evac_shift(n + QUAD - 1, (s + QUAD - 1) % SLOTS)
                evac_pv(SLOTS * i + SLOTS - 1, SLOTS - 1)

            with act.Fori(0, ITERS - 1) as i:
                attention(i, False)
            attention(ITERS - 1, True)

            with act.Fori(0, B) as b:
                for k in range(KG):
                    g = b * KG + k
                    act.wait_ge(ao_ready, KG + g + 1)
                    nc.scalar.activation(oT[:, k, :], bank(k), ACT.Copy).then_inc(ao_evac, 1)
                    act.wait_ge(x2T_ready, g + 1)
                    wait_apart(act, h2_kept, (b + 1) * KG)
                    nc.scalar.activation(hT[:, k, :], bank(4 + k), ACT.Identity,
                                         bias=mod_c[:, 3, ds(b, 1)], scale=mod_c[:, 4, ds(b, 1)]).then_inc(h2_ready, 1)
            act.wait_ge(w_chain, 1)
            nc.scalar.activation(wts[:, 1, :], wts[:, 0, :], ACT.Exp).then_inc(e_exp, 1)
            with act.Fori(0, NG) as g:
                for e in range(E):
                    for fc in range(FC):
                        n = e * FC + fc
                        act.wait_ge(h_mm, g * E * FC + n + 1)
                        if fc == 0:
                            act.wait_ge(y2_mm, g * E + e + 1)
                        nc.scalar.activation(hid[:, (e % 2) * FC + fc, :], bank(n % 4), ACT.Gelu,
                                             bias=b1c[:, n:n + 1]).then_inc(gelu_done, 1)

        @block.vector
        def _(dve):
            dve.sem_inc(o_done, 1)
            dve.sem_inc(q_split, 2)
            dve.sem_inc(k_split, 2)
            dve.sem_inc(v_evac, 2)
            dve.sem_inc(mx_free, 2)
            dve.sem_inc(y2_evac, 2)
            dve.sem_inc(g_evac, 2)
            dve.sem_inc(y_scaled, 2)
            chain = [0]

            def link(ins):
                chain[0] += 1
                ins.then_inc(dve_chain, 1)
                dve.wait_ge(dve_chain, chain[0])

            for e in range(E):
                last = nc.vector.memset(iota_e[:, e:e + 1], float(e))
            dve.wait_ge(c_exp_done, 1)
            link(nc.vector.tensor_scalar(silu_t[:, 1, :], silu_t[:, 0, :], 1.0, None, ALU.add))
            link(nc.vector.reciprocal(silu_t[:, 0, :], silu_t[:, 1, :]))
            link(nc.vector.tensor_tensor(siluT[:, :], cT[:, :], silu_t[:, 0, :], ALU.mult))
            for b in range(B):
                last = nc.vector.tensor_copy(silu_b[:, b, :], siluT[:, b:b + 1].broadcast_to([P, P]))
            last.then_inc(silu_done, 1)
            dve.wait_ge(mod_done, 1)
            modp = bank(2)[:, 0:MOD * B].rearrange("p (m b) -> p m b", b=B)
            link(nc.vector.tensor_copy(mod_c[:, :, :], modp))
            for m in (1, 4):
                last = nc.vector.tensor_scalar(mod_c[:, m, :], mod_c[:, m, :], 1.0, None, ALU.add)
            link(last)
            for n, dst in ((0, gaB), (1, gbB)):
                src = bank(3 + n)
                fl = [gate_t[:, j, :, :].rearrange("p b d -> p (b d)") for j in range(2)]
                link(nc.vector.tensor_scalar(fl[0], src, 0.0, 2.0, ALU.is_ge, ALU.mult))
                link(nc.vector.tensor_scalar(fl[1], src, -1.0, None, ALU.mult))
                link(nc.vector.tensor_tensor(fl[1], src, fl[1], ALU.max))
                link(nc.vector.tensor_scalar(fl[1], fl[1], 0.25, None, ALU.max))
                link(nc.vector.scalar_tensor_tensor(dst[:, :, :].rearrange("p b d -> p (b d)"), fl[0], -1.0, fl[1],
                                                    ALU.add, ALU.mult))
            dve.wait_ge(w_loaded, W_LOADS * 16)
            for b in range(B):
                last = nc.vector.tensor_tensor(gaboB[:, b, :], gaB[:, b, :], boB[:, :], ALU.mult)
            nc.vector.reciprocal(rtemp[:, :], tempB[:, :]).then_inc(mod_ready, 1)

            def layernorm(g, k, mv_sem, rstd_sem, xn_sem, bn_chain):
                for t in range(GT):
                    last = nc.vector.bn_stats(stats[:, k, t, :], x_sb[:, ds(g, 1), t, :].rearrange("p a d -> p (a d)"))
                last.then_inc(bn_chain, 1)
                wait_apart(dve, bn_chain, g + 1)
                for t in range(GT):
                    last = nc.vector.bn_aggr(mv[:, k, t, :], stats[:, k, t, :])
                last.then_inc(mv_sem, 1)
                dve.wait_ge(mv_sem, g + 1)
                dve.wait_ge(rstd_sem, g + 1)
                for t in range(GT):
                    last = nc.vector.tensor_scalar(
                        xn[:, k, t, :], x_sb[:, ds(g, 1), t, :].rearrange("p a d -> p (a d)"),
                        mv[:, k, t, 0:1], rstd[:, k, t:t + 1], ALU.subtract, ALU.mult)
                last.then_inc(xn_sem, 1)

            dve.wait_ge(x_loaded, 16)
            HQ = H * QT * DK
            with dve.Fori(0, B) as b:
                for k in range(KG):
                    g = b * KG + k
                    layernorm(g, k, mv_ready, rstd_ready, xn_ready, st_chain)
                    dve.wait_ge(v_mm, g + 1)
                    v_v = v_all[:, ds(b * HQ, HQ)].rearrange("p (h k d) -> p k h d", h=H, k=QT)
                    for t in range(GT):
                        last = nc.vector.tensor_tensor(
                            v_v[:, k * GT + t, :, :],
                            bank(6 + k)[:, t * D:(t + 1) * D].rearrange("p (h d) -> p h d", h=H),
                            bvB[:, :].rearrange("p (h d) -> p h d", h=H), ALU.add)
                    last.then_inc(v_evac, 1)
                    dve.wait_ge(q_evac, 2 + g + 1)
                    dve.wait_ge(q_written[k], (b + 1) * NPART * 16)
                    part = [q_parts[:, k, n, :] for n in range(NPART)]
                    nc.vector.tensor_copy(part[0], qf[:, k, :]).then_inc(qs_chain, 1)
                    dve.wait_ge(qs_chain, g * 3 + 1)
                    nc.vector.tensor_tensor(qf[:, k, :], qf[:, k, :], part[0], ALU.subtract).then_inc(qs_chain, 1)
                    dve.wait_ge(qs_chain, g * 3 + 2)
                    nc.vector.tensor_copy(part[1], qf[:, k, :]).then_inc(qs_chain, 1)
                    dve.wait_ge(qs_chain, g * 3 + 3)
                    nc.vector.tensor_tensor(part[2], qf[:, k, :], part[1], ALU.subtract).then_inc(q_split, 1)

            def reduce_max(m, s, qt):
                dve.wait_ge(mx_ready, QT * m + qt + 1)
                nc.vector.tensor_reduce(nmax[:, s, qt:qt + 1], bank(2 + 2 * (qt % 2), 2), AX.X, ALU.max,
                                        negate=True).then_inc(mx_free, 1)

            def normalise(i, s):
                n = SLOTS * i + s
                dve.wait_ge(oT_ready, n + 1)
                o_ps = bank(MISC)[:, 0:2 * P].rearrange("p (c j e) -> p c j e", c=2, j=4)
                r = rsum[:, s % 2, :, :]
                nc.vector.reciprocal(r, o_ps[:, :, :, DK]).then_inc(rsum_ready, 1)
                dve.wait_ge(rsum_ready, n + 1)
                o_v = o_all[:, ds(i * QT * SLOTS * DK, QT * SLOTS * DK)].rearrange(
                    "p (j c s d) -> p c j s d", j=4, c=2, s=SLOTS)
                nc.vector.tensor_tensor(o_v[:, :, :, s, :], o_ps[:, :, :, 0:DK],
                                        r.rearrange("p c (j a) -> p c j a", a=1).broadcast_to([P, 2, 4, DK]),
                                        ALU.mult).then_inc(o_done, 1)

            for m in range(QUAD):
                for qt in range(QT):
                    reduce_max(m, m, qt)

            def attention(i, last):
                for s in range(SLOTS):
                    for kt in range(QT):
                        if not last or s < QUAD:
                            reduce_max(SLOTS * i + s + QUAD, (s + QUAD) % SLOTS, kt)
                        if kt == 3 and s:
                            normalise(i, s - 1)
                normalise(i, SLOTS - 1)

            with dve.Fori(0, ITERS - 1) as i:
                attention(i, False)
            attention(ITERS - 1, True)

            with dve.Fori(0, B) as b:
                for k in range(KG):
                    g = b * KG + k
                    dve.wait_ge(y_mm, g + 1)
                    for t in range(GT):
                        last = nc.vector.tensor_tensor(y_sb[:, k, t, :], bank(2 + k)[:, t * D:(t + 1) * D],
                                                       gaB[:, ds(b, 1), :].rearrange("p a d -> p (a d)"), ALU.mult)
                    last.then_inc(y_scaled, 1)
                    dve.wait_ge(y_scaled, 2 + g + 1)
                    dve.wait_ge(xg_ready, g + 1)
                    xg = x_sb[:, ds(g, 1), :, :].rearrange("p a t d -> p (a t d)")
                    nc.vector.tensor_tensor(xg, y_sb[:, k, :, :].rearrange("p t d -> p (t d)"), xg,
                                            ALU.add).then_inc(x2_ready, 1)
                    wait_apart(dve, x2_ready, g + 1)
                    layernorm(g, k, mv2_ready, rstd2_ready, xn2_ready, st2_chain)
                    dve.wait_ge(g_mm, g + 1)
                    nc.vector.tensor_tensor(logits[:, k, :, :], bank(6 + k)[:, 0:GT * E].rearrange("p (t e) -> p t e", e=E),
                                            gbiasB[:, :].rearrange("p (a e) -> p a e", a=1).broadcast_to([P, GT, E]),
                                            ALU.add).then_inc(g_evac, 1)
                    dve.wait_ge(g_evac, 2 + g + 1)
                    lg = logits[:, k, :, :].rearrange("p t e -> p (t e)")
                    nc.vector.tensor_scalar(lg, lg, rtemp[:, :], None, ALU.mult).then_inc(g_chain, 1)
                    wait_apart(dve, g_chain, g * 3 + 1)
                    for t in range(GT):
                        last = nc.vector.max(eight_v[:, k, t, :], logits[:, k, t, :])
                    last.then_inc(g_chain, 1)
                    wait_apart(dve, g_chain, g * 3 + 2)
                    for t in range(GT):
                        last = nc.vector.max_index(eight_i[:, k, t, :], eight_v[:, k, t, :], logits[:, k, t, :])
                    last.then_inc(g_chain, 1)
                    dve.wait_ge(g_chain, g * 3 + 3)
                    for n in range(2):
                        nc.vector.tensor_copy(top_v[:, n, ds(g * GT, GT)], eight_v[:, k, :, n])
                        last = nc.vector.tensor_copy(top_if[:, n, ds(g * GT, GT)], eight_i[:, k, :, n])
                    last.then_inc(topi_done, 1)
            dve.wait_ge(topi_done, NG)
            nc.vector.tensor_tensor(wts[:, 0, :], top_v[:, 1, :], top_v[:, 0, :], ALU.subtract).then_inc(w_chain, 1)
            dve.wait_ge(e_exp, 1)
            link(nc.vector.tensor_scalar(wts[:, 2, :], wts[:, 1, :], 1.0, None, ALU.add))
            link(nc.vector.reciprocal(wts[:, 3, :], wts[:, 2, :]))
            link(nc.vector.tensor_tensor(wts[:, 2, :], wts[:, 1, :], wts[:, 3, :], ALU.mult))
            NT = NG * GT
            for n, w in ((0, 3), (1, 2)):
                for t in range(NT):
                    last = nc.vector.tensor_scalar(hot[:, n, t, :], iota_e[:, :], top_if[:, n, t:t + 1],
                                                   wts[:, w, t:t + 1], ALU.is_equal, ALU.mult)
            link(last)
            flat = [a.rearrange("p t e -> p (t e)") for a in (w_exp[:, :, :], hot[:, 0, :, :], hot[:, 1, :, :])]
            nc.vector.tensor_tensor(flat[0], flat[1], flat[2], ALU.add).then_inc(wexp_ready, 1)
            dve.wait_ge(wexp_ready, 1)

            with dve.Fori(0, B) as b:
                for k in range(KG):
                    g = b * KG + k
                    dve.wait_ge(out_stored[k], (b + 1) * 16)
                    c0 = g * E

                    def w_of(e, t):
                        return w_exp[:, ds(g * GT + t, 1), e:e + 1].rearrange("p a e -> p (a e)")

                    for e in range(E):
                        for t in range(GT):
                            if e == 0:
                                last = nc.vector.tensor_scalar(acc[:, k, t, :], b2B[:, e, :], w_of(e, t), None, ALU.mult)
                            else:
                                last = nc.vector.scalar_tensor_tensor(acc[:, k, t, :], b2B[:, e, :], w_of(e, t),
                                                                      acc[:, k, t, :], ALU.mult, ALU.add)
                        last.then_inc(acc_chain, 1)
                        dve.wait_ge(acc_chain, c0 + e + 1)
                    for e in range(E):
                        dve.wait_ge(y2_mm, 2 + g * E + e + 1)
                        for t in range(GT):
                            last = nc.vector.scalar_tensor_tensor(
                                acc[:, k, t, :], bank(4 + e % 2)[:, t * D:(t + 1) * D], w_of(e, t),
                                acc[:, k, t, :], ALU.mult, ALU.add)
                        last.then_inc(y2_evac, 1)
                        dve.wait_ge(y2_evac, 2 + g * E + e + 1)
                    for t in range(GT):
                        last = nc.vector.tensor_tensor(acc[:, k, t, :], acc[:, k, t, :],
                                                       gbB[:, ds(b, 1), :].rearrange("p a d -> p (a d)"), ALU.mult)
                    last.then_inc(fin_chain, 1)
                    dve.wait_ge(fin_chain, g + 1)
                    a = acc[:, k, :, :].rearrange("p t d -> p (t d)")
                    nc.vector.tensor_tensor(a, a, x_sb[:, ds(g, 1), :, :].rearrange("p a t d -> p (a t d)"),
                                            ALU.add).then_inc(out_ready, 1)

        @block.tensor
        def _(pe):
            mm = nc.tensor.matmul
            pe.sem_inc(pv_done, RING)
            pe.sem_inc(y2_mm, 2)
            pe.sem_inc(ao_ready, KG)
            pe.wait_ge(ident_made, 2)
            pe.wait_ge(w_loaded, W_LOADS * 16)
            for n in range(4):
                nc.tensor.transpose(bank(0)[:, n * D:(n + 1) * D], w_raw[:, n, :], ident[:, :])
            nc.tensor.transpose(bank(1)[:, 0:E * FC], b1_raw[:, :], ident[0:E * FC, 0:E * FC]).then_inc(w_transposed, 1)
            pe.wait_ge(silu_done, 1)
            for m in range(MOD):
                mm(bank(2)[:, m * B:(m + 1) * B], wmod[:, m * D:(m + 1) * D], siluT[:, :], start=True, stop=True)
            for n, m in ((0, 2), (1, 5)):
                for b in range(B):
                    last = mm(bank(3 + n)[:, b * D:(b + 1) * D], silu_b[:, b, :], wmod[:, m * D:(m + 1) * D],
                              start=True, stop=True)
            last.then_inc(mod_done, 1)
            pe.wait_ge(wT_ready, 2)
            pe.wait_ge(mod_ready, 1)

            with pe.Fori(0, B) as b:
                for k in range(KG):
                    g = b * KG + k
                    pe.wait_ge(xn_ready, g + 1)
                    pe.wait_ge(hT_ready, g + 1)
                    for t in range(GT):
                        last = nc.tensor.transpose(bank(k)[:, t * P:(t + 1) * P], xn[:, k, t, :], ident[:, :])
                    last.then_inc(xT_ready, 1)
                    pe.wait_ge(hT_ready, 2 + g + 1)
                    pe.wait_ge(q_evac, g + 1)
                    mm(bank(2 + k), wT[:, 0, :], hT[:, k, :], start=True, stop=True).then_inc(q_mm, 1)
                    pe.wait_ge(k_evac, g + 1)
                    mm(bank(4 + k), wT[:, 1, :], hT[:, k, :], start=True, stop=True).then_inc(k_mm, 1)
                    pe.wait_ge(v_evac, g + 1)
                    for t in range(GT):
                        last = mm(bank(6 + k)[:, t * D:(t + 1) * D], hT[:, k, t * P:(t + 1) * P], wT[:, 2, :],
                                  start=True, stop=True)
                    last.then_inc(v_mm, 1)
            pe.wait_ge(q_evac, 2 + NG)
            pe.wait_ge(k_evac, 2 + NG)
            pe.wait_ge(v_evac, 2 + NG)

            def scores_for_max(i, s, m, qt):
                if qt == 0:
                    pe.wait_ge(q_loaded[s], 3 * 16 * (i + 1))
                    pe.wait_ge(k_loaded[s // 2], 2 * PAIRS * 16 * (i + 1))
                pe.wait_ge(mx_free, QT * m + qt + 1)
                for half in range(2):
                    last = mm(bank(2 + 2 * (qt % 2) + half), q_stack[0:SHIFT, s, qt * P:(qt + 1) * P],
                              k_stack[0:SHIFT, s // 2, half * 512:(half + 1) * 512], start=True, stop=True)
                last.then_inc(mx_ready, 1)

            def transpose_shift(m, s, o_count):
                pe.wait_ge(nmax_split, m + 1)
                pe.wait_ge(nmaxT_evac, 1 + m)
                pe.wait_ge(o_done, 1 + o_count)
                nc.tensor.transpose(bank(MISC)[0:NPART * QT, 0:P // 2].bitcast(BF16),
                                    nmax_p[:, s, :, :].rearrange("p n t -> p (n t)"), ident_b[:, :])\
                  .then_inc(nmaxT_ready, 1)

            def transpose_out(n, s, shift_count):
                pe.wait_ge(pv_evac, 1 + n + 1)
                pe.wait_ge(nmaxT_evac, 1 + shift_count)
                pe.wait_ge(o_done, 1 + n)
                for c in range(2):
                    last = nc.tensor.transpose(bank(MISC)[:, c * P:(c + 1) * P], pv_sb[:, s % 2, c * P:(c + 1) * P],
                                               ident[:, :])
                last.then_inc(oT_ready, 1)

            def pv(i, s, kt):
                n = SLOTS * i + s
                pe.wait_ge(exp_done, 2 + 16 * n + 2 * kt + 2)
                if kt == 0:
                    pe.wait_ge(pv_evac, n + 1)
                    if s % QUAD == 0:
                        pe.wait_ge(v_staged, 2 * i + s // QUAD + 1)
                for j in range(4):
                    last = mm(bank(PV)[32 * j:32 * j + 32, 0:2 * P], v_stage[:, s, kt, :],
                              probs[:, kt % RING, j * 2 * P:(j + 1) * 2 * P], start=kt == 0, stop=kt == QT - 1)
                last.then_inc(pv_done, 1)

            pe.wait_ge(stacks_cleared, 3)
            for m in range(QUAD):
                for qt in range(QT):
                    scores_for_max(0, m, m, qt)
                if m:
                    transpose_shift(m - 1, m - 1, 0)

            def attention(i, last):
                for s in range(SLOTS):
                    n = SLOTS * i + s
                    for kt in range(QT):
                        if kt == 0:
                            pe.wait_ge(shift_loaded[s], 16 * (i + 1))
                        for half in range(2):
                            pe.wait_ge(exp_done, 16 * n + 2 * kt + half + 1)
                            mm(bank(half), k_stack[0:KROWS, s // 2, kt * P:(kt + 1) * P],
                               q_stack[0:KROWS, s, half * 512:(half + 1) * 512], start=True, stop=True)\
                              .then_inc(st_ready, 1)
                        if not last or s < QUAD:
                            scores_for_max(i + (s + QUAD) // SLOTS, (s + QUAD) % SLOTS, n + QUAD, kt)
                        if kt:
                            pv(i, s, kt - 1)
                        shifts = SLOTS * i + s + QUAD - 1
                        if kt == 2 and s:
                            transpose_out(n - 1, s - 1, min(shifts, B * H) if last else shifts)
                        if kt == 4 and (not last or s <= QUAD):
                            transpose_shift(n + QUAD - 1, (s + QUAD - 1) % SLOTS, n)
                    pv(i, s, QT - 1)
                shifts = SLOTS * i + SLOTS + QUAD - 1
                transpose_out(SLOTS * i + SLOTS - 1, SLOTS - 1, min(shifts, B * H) if last else shifts)

            with pe.Fori(0, ITERS - 1) as i:
                attention(i, False)
            attention(ITERS - 1, True)
            pe.wait_ge(o_done, 1 + B * H)

            with pe.Fori(0, B) as b:
                for k in range(KG):
                    g = b * KG + k
                    pe.wait_ge(o_staged, g + 1)
                    pe.wait_ge(ao_evac, g + 1)
                    for t in range(GT):
                        last = nc.tensor.transpose(bank(k)[:, t * P:(t + 1) * P], o_st[:, k, t * D:(t + 1) * D],
                                                   ident[:, :])
                    last.then_inc(ao_ready, 1)
                    pe.wait_ge(ao_evac, 2 + g + 1)
                    pe.wait_ge(y_scaled, g + 1)
                    for t in range(GT):
                        last = mm(bank(2 + k)[:, t * D:(t + 1) * D], oT[:, k, t * P:(t + 1) * P], wT[:, 3, :],
                                  start=True, stop=True)
                    last.then_inc(y_mm, 1)
                    pe.wait_ge(xn2_ready, g + 1)
                    pe.wait_ge(h2_ready, g + 1)
                    for t in range(GT):
                        last = nc.tensor.transpose(bank(4 + k)[:, t * P:(t + 1) * P], xn[:, k, t, :], ident[:, :])
                    last.then_inc(x2T_ready, 1)
                    pe.wait_ge(h2_ready, 2 + g + 1)
                    pe.wait_ge(g_evac, g + 1)
                    for t in range(GT):
                        last = mm(bank(6 + k)[:, t * E:(t + 1) * E], hT[:, k, t * P:(t + 1) * P], gate_w[:, :],
                                  start=True, stop=True)
                    last.then_inc(g_mm, 1)
            pe.wait_ge(g_evac, 2 + NG)
            pe.wait_ge(h2_kept, KG + NG)
            pe.wait_ge(ffn_loaded, 32)

            def down(g, e):
                pe.wait_ge(gelu_done, 4 + (g * E + e + 1) * FC)
                pe.wait_ge(y2_evac, g * E + e + 1)
                for t in range(GT):
                    for fc in range(FC):
                        last = mm(bank(4 + e % 2)[:, t * D:(t + 1) * D],
                                  hid[:, (e % 2) * FC + fc, t * P:(t + 1) * P], w2[:, e * FC + fc, :],
                                  start=fc == 0, stop=fc == FC - 1)
                last.then_inc(y2_mm, 1)

            with pe.Fori(0, NG) as g:
                for e in range(E):
                    for fc in range(FC):
                        n = e * FC + fc
                        pe.wait_ge(gelu_done, g * E * FC + n + 1)
                        mm(bank(n % 4), w1[:, e, fc * P:(fc + 1) * P], h2T_all[:, ds(g * G, G)],
                           start=True, stop=True).then_inc(h_mm, 1)
                    if e:
                        down(g, e - 1)
                down(g, E - 1)


_INS = ["L0_attn_x", "L0_attn_Wq", "L0_attn_bq", "L0_attn_Wk", "L0_attn_bk", "L0_attn_Wv", "L0_attn_bv",
        "L0_attn_Wo", "L0_attn_bo", "L0_ffn_W1", "L0_ffn_b1", "L0_ffn_W2", "L0_ffn_b2", "L0_ffn_gate_w",
        "L0_ffn_gate_b", "L0_ffn_temperature", "L0_c", "L0_wmod"]


def kernel(**inputs):
    import numpy as _np
    import concourse.bacc as _bacc
    from concourse import mybir as _mybir
    from concourse.bass_utils import run_bass_kernel_spmd as _run

    nc = _bacc.Bacc("TRN2", target_bir_lowering=False, num_devices=1)
    arrays, args = {}, []
    for name in _INS:
        a = _np.ascontiguousarray(inputs[name])
        if name == "L0_ffn_temperature":
            a = a.reshape(1)
        arrays[f"in_{name}"] = a
        args.append(nc.dram_tensor(f"in_{name}", a.shape, _mybir.dt.from_np(a.dtype), kind="ExternalInput").ap())
    shape = inputs["L0_attn_x"].shape
    out = nc.dram_tensor("out_0", shape, _mybir.dt.float32, kind="ExternalOutput").ap()
    adaln_block(nc, *args, out)
    r = _run(nc, [arrays], core_ids=[0])
    return r.results[0]["out_0"]
```

```python
from contextlib import ExitStack

import concourse.bass as bass
import numpy as np
from concourse import mybir


def adaln_block(nc, x_d, wq_d, bq_d, wk_d, bk_d, wv_d, bv_d, wo_d, bo_d,
                w1_d, b1_d, w2_d, b2_d, gw_d, gb_d, temp_d, c_d, wmod_d, out_d):
    F32, BF16, U32, F32R = mybir.dt.float32, mybir.dt.bfloat16, mybir.dt.uint32, mybir.dt.float32r
    ALU, ACT, AX = mybir.AluOpType, mybir.ActivationFunctionType, mybir.AxisListType
    ds = bass.ds

    P = 128
    B, S, D = x_d.shape
    E, _, F = w1_d.shape
    H, DK = 16, D // 16
    MOD = 6
    G = 512
    GT = G // P
    KG = S // G
    NG = B * KG
    QT = S // P
    FC = F // P
    SLOTS = 8
    ITERS = B * H // SLOTS
    AHEAD = 2
    QUAD = 4
    NPART = 3
    PAIRS = 6
    ROWS = PAIRS * DK
    SHIFT = 2 * ROWS
    NT = B * QT
    KROWS = SHIFT + NPART
    HW = 16
    OUTS = B * H // 2
    RING = 4
    PV, MISC = 6, 7
    W_LOADS = 13
    SCALE = 1.0 / float(np.sqrt(DK))
    EPS = 1e-5

    ctx = ExitStack()
    with ctx:
        def sb(name, shape, dt=F32):
            return ctx.enter_context(nc.sbuf_tensor(name, shape, dt))

        def sem(name):
            return ctx.enter_context(nc.semaphore(name))

        x_sb = sb("x_sb", [P, NG, GT, D])
        w1 = sb("w1", [P, 2, E, F], F32R)
        w2 = sb("w2", [P, 2, E, FC * D], F32R)
        wT = sb("wT", [P, 4, D])
        ident = sb("ident", [P, P])
        ident_b = sb("ident_b", [P, P], BF16)
        cT = sb("cT", [P, B])
        silu_t = sb("silu_t", [P, 2, B])
        siluT = sb("siluT", [P, B])
        mod_c = sb("mod_c", [P, MOD, B])
        gaB = sb("gaB", [P, B, D])
        gaboB = sb("gaboB", [P, B, D])
        gbiasB = sb("gbiasB", [P, E])
        tempB = sb("tempB", [P, 1])
        rtemp = sb("rtemp", [P, 1])
        b1c = sb("b1c", [P, E * FC])
        bq = sb("bq", [P, 1])
        bk = sb("bk", [P, 1])
        gate_w = sb("gate_w", [P, E])
        mhalf = sb("mhalf", [P, NT])
        to_rows = sb("to_rows", [P, 2, 2 * HW])
        stats = sb("stats", [P, NT, 6])
        mean = sb("mean", [P, NT])
        var = sb("var", [P, 4, NT])
        vareps = sb("vareps", [P, NT])
        rstd = sb("rstd", [P, NT])
        xn = sb("xn", [P, KG, GT, D])
        hT = sb("hT", [P, KG, G])
        qf = sb("qf", [P, KG, G])
        kf = sb("kf", [P, KG, G])
        o_st = qf
        oT = kf
        y_sb = xn
        iota_e = sb("iota_e", [P, E])
        b2c = sb("b2c", [P, E])
        gb_c = sb("gb_c", [P, 3, B])

        def placed_in(stack):
            return lambda name, shape, dt=F32: stack.enter_context(nc.sbuf_tensor(name, shape, dt))

        with ExitStack() as attention_phase:
            sa = placed_in(attention_phase)
            o_all = sa("o_all", [P, OUTS, GT, KG, 2 * DK])
            v_all = sa("v_all", [P, B * H * QT * DK])
            q_stack = sa("q_stack", [P, SLOTS, S], BF16)
            k_stack = sa("k_stack", [P, SLOTS // 2, S], BF16)
            v_stage = sa("v_stage", [P, SLOTS, QT, 32])
            rsum = sa("rsum", [P, 2, 4 * QT // 2])
            nmax = sa("nmax", [P, SLOTS, QT])
            nmax_r = sa("nmax_r", [P, SLOTS, 2, QT])
            nmax_p = sa("nmax_p", [P, SLOTS, NPART, QT], BF16)
            nmaxT = sa("nmaxT", [NPART * QT, SLOTS, P], BF16)
            with ExitStack() as start_phase:
                ss = placed_in(start_phase)
                w_raw = ss("w_raw", [P, 4, D])
                wmod = ss("wmod", [P, MOD * D])
                silu_b = ss("silu_b", [P, B, P])
                gate_t = ss("gate_t", [P, 2, B, D])
                q_parts = ss("q_parts", [P, KG, NPART, G], BF16)
                k_parts = ss("k_parts", [P, KG, NPART, G], BF16)
                bvB = ss("bvB", [P, D])
                boB = ss("boB", [P, D])
                b2_raw = ss("b2_raw", [E, D])
                b1_raw = ss("b1_raw", [E * FC, P])
            probs = sa("probs", [P, RING, S])
            w12_raw = sa("w12_raw", [P, 2, F])
            pv_sb = sa("pv_sb", [P, 2, G])
        with ExitStack() as ffn_phase:
            sf = placed_in(ffn_phase)
            h2 = sf("h2", [P, 2, NG * G], F32R)
            w_exp = sf("w_exp", [P, NG * GT, E])
            sel = sf("sel", [P, E, P], BF16)
            wT_parts = sf("wT_parts", [P, NT * P], BF16)
            wts = sf("wts", [P, 4, NG * GT])
            top_if = sf("top_if", [P, 2, NG * GT])
            acc = sf("acc", [P, G])
            acc_t = sf("acc_t", [P, G])
            acc_gb = sf("acc_gb", [P, G])
            w_bc = sf("w_bc", [P, 2, G])
            out_sb = sf("out_sb", [P, GT, D])
            with ExitStack() as routing_phase:
                sr = placed_in(routing_phase)
                w_parts = sr("w_parts", [P, NT, NPART, E], BF16)
                w_rest = sr("w_rest", [P, 2, NT, E])
                hot = sr("hot", [P, 2, NG * GT, E])
                eight_v = sr("eight_v", [P, NT, 8])
                eight_i = sr("eight_i", [P, NT, 8], U32)
                logits = sr("logits", [P, NT, E])
            hid = sf("hid", [P, FC, G])
            hid_hl = sf("hid_hl", [P, 2, 2 * FC, G], F32R)

        psum = ctx.enter_context(nc.psum_tensor("psum", [P, 8 * 512], F32))

        def bank(n, k=1):
            return psum[:, n * 512:(n + k) * 512]

        q_dram = nc.dram_tensor("q_dram", (B * H, DK, NPART, S), BF16, kind="Internal").ap()
        k_dram = nc.dram_tensor("k_dram", (B * H, DK, NPART, S), BF16, kind="Internal").ap()

        x_loaded = [sem(f"x_loaded{half}") for half in range(2)]
        small_loaded, w_loaded = sem("small_loaded"), sem("w_loaded")
        consts_made, ident_made, stacks_cleared = sem("consts_made"), sem("ident_made"), sem("stacks_cleared")
        pool_chain, dve_chain = sem("pool_chain"), sem("dve_chain")
        c_exp_done, silu_done, mod_done, mod_ready, w_transposed, wT_ready = (
            sem(n) for n in ("c_exp_done", "silu_done", "mod_done", "mod_ready", "w_transposed", "wT_ready"))
        stats_done, var_ready, rstd_ready, xn_ready, xT_ready, hT_ready = (
            sem(n) for n in ("stats_done", "var_ready", "rstd_ready", "xn_ready", "xT_ready", "hT_ready"))
        q_mm, k_mm, v_mm, q_evac, k_evac, v_evac, q_split, k_split = (
            sem(n) for n in ("q_mm", "k_mm", "v_mm", "q_evac", "k_evac", "v_evac", "q_split", "k_split"))
        q_written = [sem(f"q_written{k}") for k in range(KG)]
        k_written = [sem(f"k_written{k}") for k in range(KG)]
        q_loaded = [sem(f"q_loaded{s}") for s in range(SLOTS)]
        k_loaded = [sem(f"k_loaded{s}") for s in range(SLOTS // 2)]
        shift_loaded = [sem(f"shift_loaded{s}") for s in range(SLOTS)]
        st_ready, exp_done, mx_ready, mx_free, k_chain, nmax_split, nmaxT_ready, nmaxT_evac = (
            sem(n) for n in ("st_ready", "exp_done", "mx_ready", "mx_free", "k_chain", "nmax_split", "nmaxT_ready", "nmaxT_evac"))
        pv_done, pv_evac, oT_ready, rsum_ready, o_done, v_staged = (
            sem(n) for n in ("pv_done", "pv_evac", "oT_ready", "rsum_ready", "o_done", "v_staged"))
        o_staged, xg_ready, ao_ready, ao_evac, y_mm, y_scaled, x2_ready = (
            sem(n) for n in ("o_staged", "xg_ready", "ao_ready", "ao_evac", "y_mm", "y_scaled", "x2_ready"))
        xn2_ready, x2T_ready, h2_ready, h2_kept, g_mm, g_evac = (
            sem(n) for n in ("xn2_ready", "x2T_ready", "h2_ready", "h2_kept", "g_mm", "g_evac"))
        g_chain, w_chain, e_exp, wexp_ready = sem("g_chain"), sem("w_chain"), sem("e_exp"), sem("wexp_ready")
        h_mm, gelu_done, y2_mm, y2_evac, acc_chain, out_ready = (
            sem(n) for n in ("h_mm", "gelu_done", "y2_mm", "y2_evac", "acc_chain", "out_ready"))
        out_stored, w12_loaded, w_split, h2_low = sem("out_stored"), sem("w12_loaded"), sem("w_split"), sem("h2_low")
        wp_ready, wpT_ready, wpT_evac, wb_mm, wb_evac, low_pool, low_dve, gated, outT_mm, sel_ready = (
            sem(n) for n in ("wp_ready", "wpT_ready", "wpT_evac", "wb_mm", "wb_evac", "low_pool", "low_dve", "gated",
                             "outT_mm", "sel_ready"))
        ws_chain = sem("ws_chain")
        qs_chain, sm_chain, fin_chain = sem("qs_chain"), sem("sm_chain"), sem("fin_chain")

        waits_apart = sem("waits_apart")

        def wait_apart(eng, semaphore, value):
            eng.wait_ge(semaphore, value)
            eng.sem_inc(waits_apart, 1)

        block = ctx.enter_context(nc.Block())
        x_v = x_d.rearrange("b s d -> (b s) d").rearrange("(g p t) d -> g p t d", p=P, t=GT)
        out_v = out_d.rearrange("b s d -> (b s) d").rearrange("(g p t) d -> g p t d", p=P, t=GT)

        @block.sync
        def _(sp):
            sp.sem_inc(out_stored, 16)
            for k in range(KG):
                sp.sem_inc(q_written[k], 16)
                sp.sem_inc(k_written[k], 16)
            sp.dma_start(cT[:, :], c_d.rearrange("b d -> d b"), allow_slow_non_contiguous=True).then_inc(small_loaded, 16)
            sp.dma_start(wmod[:, :], wmod_d).then_inc(small_loaded, 16)
            for half in range(2):
                part = slice(half * NG // 2, (half + 1) * NG // 2)
                sp.dma_start(x_sb[:, part, :, :], x_v[part].rearrange("g p t d -> p g (t d)"))\
                  .then_inc(x_loaded[half], 16)
            for n, w in enumerate((wq_d, wk_d, wv_d, wo_d)):
                sp.dma_start(w_raw[:, n, :], w).then_inc(w_loaded, 16)
            for dst, src in ((bq, bq_d), (bk, bk_d)):
                sp.dma_start(dst[:, :], src.rearrange("(d a) -> d a", a=1), allow_slow_non_contiguous=True).then_inc(w_loaded, 16)
            for dst, src in ((bvB[:, :], bv_d), (boB[:, :], bo_d), (gbiasB[:, :], gb_d)):
                sp.dma_start(dst, src.partition_broadcast(P)).then_inc(w_loaded, 16)
            sp.dma_start(tempB[:, :], temp_d.partition_broadcast(P)).then_inc(w_loaded, 16)
            sp.dma_start(gate_w[:, :], gw_d).then_inc(w_loaded, 16)
            sp.dma_start(b1_raw[:, :], b1_d.rearrange("e (c f) -> (e c) f", f=P)).then_inc(w_loaded, 16)
            sp.dma_start(b2_raw[:, :], b2_d).then_inc(w_loaded, 16)
            def store_parts(g):
                b, k = g // KG, g % KG
                for split, parts, dram, written in ((q_split, q_parts, q_dram, q_written),
                                                    (k_split, k_parts, k_dram, k_written)):
                    sp.wait_ge(split, 2 + g + 1)
                    rows = dram[b * H:(b + 1) * H, :, :, k * G:(k + 1) * G]
                    sp.dma_start(rows.rearrange("h d n t -> (h d) n t"), parts[:, k, :, :]).then_inc(written[k], 16)

            STACK = [(0, 3, 0), (3, 2, 1), (5, 1, 2)]

            def load_q(i, s):
                r = (s % 2) * ROWS
                for at, n, _ in STACK:
                    src = q_dram[ds(i * SLOTS + s, 1), :, 0:n, :].rearrange("a d n t -> (a d) n t")
                    sp.dma_start(q_stack[r + at * DK:r + (at + n) * DK, s, :], src).then_inc(q_loaded[s], 16)

            def load_k(i, s):
                r = (s % 2) * ROWS
                for at, n, part in STACK:
                    src = k_dram[ds(i * SLOTS + s, 1), :, part:part + 1, :].rearrange("a d n t -> (a d) n t")
                    sp.dma_start(k_stack[r + at * DK:r + (at + n) * DK, s // 2, :],
                                 src.broadcast_to([DK, n, S])).then_inc(k_loaded[s // 2], 16)

            for g in range(NG):
                store_parts(g)
                if g == KG:
                    sp.wait_ge(stacks_cleared, 3)
                    for k in range(KG):
                        sp.wait_ge(q_written[k], 2 * 16)
                        sp.wait_ge(k_written[k], 2 * 16)
                if g >= KG:
                    load_q(0, g - KG)
                    load_k(0, g - KG)
            for s in range(NG - KG, SLOTS):
                load_q(0, s)
                load_k(0, s)
            for k in range(KG):
                sp.wait_ge(q_written[k], (B + 1) * 16)
                sp.wait_ge(k_written[k], (B + 1) * 16)

            def store_shift(m_count, s):
                sp.wait_ge(nmaxT_evac, 1 + m_count)
                sp.dma_start(q_stack[SHIFT:KROWS, s, :], nmaxT[:, s, :]).then_inc(shift_loaded[s], 16)

            for s in range(AHEAD - 1):
                store_shift(s + 1, s)

            def attention(i, first=False, last=False):
                for s in range(SLOTS):
                    if s == 0:
                        for n, src in enumerate((w1_d[ds(i, 1), :, :].rearrange("e d f -> (e d) f"),
                                                 w2_d[ds(i, 1), :, :].rearrange("e (c f) d -> (e f) c d", f=P))):
                            dst = w12_raw[:, n, :]
                            sp.wait_ge(w_split, i + 1)
                            sp.dma_start(dst if n == 0 else dst.rearrange("p (c d) -> p c d", c=FC), src)\
                              .then_inc(w12_loaded, 16)
                    if not last or s <= SLOTS - AHEAD:
                        store_shift(SLOTS * i + s + AHEAD, (s + AHEAD - 1) % SLOTS)
                    if not last:
                        sp.wait_ge(st_ready, SLOTS * 16 * i + 16 * (s + 1))
                        load_q(i + 1, s)
                        if s % 2:
                            load_k(i + 1, s - 1)
                            load_k(i + 1, s)

            attention(0, first=True)
            with sp.Fori(1, ITERS - 1) as i:
                attention(i)
            attention(ITERS - 1, last=True)

            with sp.Fori(0, NG) as g:
                sp.wait_ge(out_ready, 1 + g + 1)
                sp.dma_start(out_v[ds(g, 1), :, :, :].rearrange("g p t d -> (g p) (t d)"),
                             out_sb[:, :, :].rearrange("p t d -> p (t d)")).then_inc(out_stored, 16)
            sp.wait_ge(out_stored, (NG + 1) * 16)

        @block.gpsimd
        def _(pool):
            pool.sem_inc(h2_low, KG)
            pool.sem_inc(w_split, 1)
            pool.sem_inc(low_pool, FC - 1)
            chain = [0]

            def link(ins):
                chain[0] += 1
                ins.then_inc(pool_chain, 1)
                pool.wait_ge(pool_chain, chain[0])

            link(nc.gpsimd.memset(ident[:, :], 0.0))
            link(nc.gpsimd.memset(ident_b[:, :], 0.0))
            for m in (ident, ident_b):
                nc.gpsimd.affine_select(out=m[:, :], in_=m[:, :], compare_op=ALU.not_equal, fill=1.0,
                                        base=0, pattern=[[-1, P]], channel_multiplier=1).then_inc(ident_made, 1)
            pool.wait_ge(ident_made, 2)
            link(nc.gpsimd.memset(to_rows[:, :, :], 0.0))
            for c in range(2):
                link(nc.gpsimd.affine_select(out=to_rows[:, :, :], in_=to_rows[:, :, :], compare_op=ALU.not_equal,
                                             fill=1.0, base=-2 * 32 * c, pattern=[[-32, 2], [-1, 2 * HW]],
                                             channel_multiplier=1))
            nc.gpsimd.memset(mhalf[:, :], -0.5).then_inc(consts_made, 1)
            pool.wait_ge(consts_made, 1)
            for n, (part, value) in enumerate(((q_stack[:, :, :], 0.0), (k_stack[SHIFT:P, :, :], 1.0),
                                               (v_stage[:, :, :, :], 0.0))):
                nc.gpsimd.memset(part, value).then_inc(stacks_cleared, 1)
                pool.wait_ge(stacks_cleared, n + 1)
            for s in range(SLOTS):
                one = (s % 2) * HW + DK
                last = nc.gpsimd.memset(v_stage[:, s, :, one:one + 1], 1.0)
            link(last)


            def rstd_of(count):
                pool.wait_ge(var_ready, count)
                link(nc.gpsimd.tensor_scalar(vareps[:, :], var[:, 3, :], EPS, None, ALU.add))
                for part in (slice(0, KG * GT), slice(KG * GT, NT)):
                    nc.gpsimd.tensor_tensor(rstd[:, part], vareps[:, part], mhalf[:, part],
                                            ALU.pow).then_inc(rstd_ready, 1)

            rstd_of(1)
            with pool.Fori(0, B) as b:
                for k in range(KG):
                    g = b * KG + k
                    pool.wait_ge(k_evac, 2 + g + 1)
                    pool.wait_ge(k_written[k], (b + 1) * 16)
                    part = [k_parts[:, k, n, :] for n in range(NPART)]
                    nc.gpsimd.tensor_tensor(kf[:, k, :], kf[:, k, :], part[0], ALU.subtract).then_inc(k_chain, 1)
                    wait_apart(pool, k_chain, g * 2 + 1)
                    nc.gpsimd.tensor_copy(part[1], kf[:, k, :]).then_inc(k_chain, 1)
                    pool.wait_ge(k_chain, g * 2 + 2)
                    nc.gpsimd.tensor_tensor(part[2], kf[:, k, :], part[1], ALU.subtract).then_inc(k_split, 1)

            def stage_v(i, quad, pv_count):
                wait_apart(pool, pv_done, pv_count)
                W = QUAD * QT * DK
                v_v = v_all[:, ds(i * 2 * W + quad * W, W)].rearrange("p (s a k d) -> p a s k d", a=2, k=QT, d=DK)
                for a in range(2):
                    ins = nc.gpsimd.tensor_copy(v_stage[:, quad * QUAD + a:(quad + 1) * QUAD:2, :, a * HW:a * HW + DK],
                                                v_v[:, a, :, :, :])
                ins.then_inc(v_staged, 1)

            def split_max(m, s):
                wait_apart(pool, mx_free, 2 + QT * (m + 1))
                r1, r2 = nmax_r[:, s, 0, :], nmax_r[:, s, 1, :]
                part = [nmax_p[:, s, n, :] for n in range(NPART)]
                nc.gpsimd.tensor_copy(part[0], nmax[:, s, :]).then_inc(sm_chain, 1)
                wait_apart(pool, sm_chain, 4 * m + 1)
                nc.gpsimd.tensor_tensor(r1, nmax[:, s, :], part[0], ALU.subtract).then_inc(sm_chain, 1)
                wait_apart(pool, sm_chain, 4 * m + 2)
                nc.gpsimd.tensor_copy(part[1], r1).then_inc(sm_chain, 1)
                wait_apart(pool, sm_chain, 4 * m + 3)
                nc.gpsimd.tensor_tensor(r2, r1, part[1], ALU.subtract).then_inc(sm_chain, 1)
                wait_apart(pool, sm_chain, 4 * m + 4)
                nc.gpsimd.tensor_copy(part[2], r2).then_inc(nmax_split, 1)

            pool.wait_ge(v_evac, 2 + NG)
            stage_v(0, 0, RING)
            for m in range(AHEAD):
                split_max(m, m)

            def attention(i, first=False, last=False):
                for s in range(SLOTS):
                    if s == 0:
                        stage_v(i, 1, RING + QT * SLOTS * i)
                    if not last or s < SLOTS - AHEAD:
                        split_max(SLOTS * i + s + AHEAD, (s + AHEAD) % SLOTS)
                    if s == 2:
                        for t in range(GT):
                            xt = x_sb[:, ds(i, 1), t, :].rearrange("p a d -> p (a d)")
                            ins = nc.gpsimd.tensor_tensor(
                                xt, xt, gaboB[:, ds(i // KG, 1), :].rearrange("p a d -> p (a d)"), ALU.add)
                        ins.then_inc(xg_ready, 1)
                    if s == 5:
                        pool.wait_ge(w12_loaded, 32 * (i + 1))
                        for n, w in enumerate((w1, w2)):
                            high, low = (w[:, j, ds(i, 1), :].rearrange("p a f -> p (a f)") for j in range(2))
                            nc.gpsimd.tensor_copy(high, w12_raw[:, n, :]).then_inc(ws_chain, 1)
                            pool.wait_ge(ws_chain, 2 * i + n + 1)
                            ins = nc.gpsimd.tensor_tensor(low, w12_raw[:, n, :], high.bitcast(F32), ALU.subtract)
                        ins.then_inc(w_split, 1)
                    if s == QUAD and not last:
                        stage_v(i + 1, 0, RING + QT * (SLOTS * i + QUAD))

            attention(0, first=True)
            with pool.Fori(1, ITERS - 1) as i:
                attention(i)
            attention(ITERS - 1, last=True)

            HALF_OUTS = H // 2
            pool.wait_ge(o_done, 1 + OUTS)
            with pool.Fori(0, B) as b:
                for k in range(KG):
                    g = b * KG + k
                    wait_apart(pool, ao_ready, (b + 1) * KG)
                    for t in range(GT):
                        last = nc.gpsimd.tensor_copy(
                            o_st[:, k, t * D:(t + 1) * D].rearrange("p (a e) -> p a e", a=HALF_OUTS),
                            o_all[:, ds(b * HALF_OUTS, HALF_OUTS), t, k, :])
                    last.then_inc(o_staged, 1)
            rstd_of(2)
            with pool.Fori(0, B) as b:
                for k in range(KG):
                    g = b * KG + k
                    pool.wait_ge(h2_ready, 2 + g + 1)
                    one = [h2[:, j, ds(g * G, G)] for j in range(2)]
                    nc.gpsimd.tensor_tensor(one[1], hT[:, k, :], one[0].bitcast(F32), ALU.subtract).then_inc(h2_low, 1)
            link(nc.gpsimd.memset(sel[:, :, :], 0.0))
            for n in range(NPART):
                link(nc.gpsimd.affine_select(out=sel[:, :, :], in_=sel[:, :, :], compare_op=ALU.not_equal, fill=1.0,
                                             base=-n * E, pattern=[[-1, E], [0, P]], channel_multiplier=1))
            nc.gpsimd.memset(wT_parts[:, :], 0.0).then_inc(sel_ready, 1)
            with pool.Fori(0, NG) as g:
                for e in range(E):
                    for fc in range(FC - 1):
                        pool.wait_ge(gelu_done, 4 + (g * E + e) * FC + fc + 1)
                        u = (e % 2) * FC + fc
                        nc.gpsimd.tensor_tensor(hid_hl[:, 1, u, :], hid[:, fc, :], hid_hl[:, 0, u, :].bitcast(F32),
                                                ALU.subtract).then_inc(low_pool, 1)

        @block.scalar
        def _(act):
            act.sem_inc(hT_ready, 2)
            act.sem_inc(q_evac, 2)
            act.sem_inc(k_evac, 2)
            act.sem_inc(exp_done, 2)
            act.sem_inc(pv_evac, 1)
            act.sem_inc(nmaxT_evac, 1)
            act.sem_inc(h2_ready, 2)
            act.sem_inc(ao_evac, 2)
            act.sem_inc(gelu_done, 4)
            act.sem_inc(wb_evac, 1)
            act.sem_inc(gated, 1)
            act.wait_ge(small_loaded, 32)
            nc.scalar.activation(silu_t[:, 0, :], cT[:, :], ACT.Exp, scale=-1.0).then_inc(c_exp_done, 1)
            act.wait_ge(w_transposed, 1)
            nc.scalar.activation(wT[:, :, :].rearrange("p a b -> p (a b)"), bank(0), ACT.Copy).then_inc(wT_ready, 1)
            nc.scalar.activation(b1c[:, :], bank(1)[:, 0:E * FC], ACT.Copy).then_inc(wT_ready, 1)
            nc.scalar.activation(b2c[:, :], bank(1)[:, E * FC:E * FC + E], ACT.Copy).then_inc(wT_ready, 1)
            act.wait_ge(mod_ready, 1)
            act.wait_ge(w_loaded, W_LOADS * 16)

            def modulate(g, k, b):
                wait_apart(act, xT_ready, 2 + g + 1)
                nc.scalar.activation(hT[:, k, :], bank(k), ACT.Identity,
                                     bias=mod_c[:, 0, ds(b, 1)], scale=mod_c[:, 1, ds(b, 1)]).then_inc(hT_ready, 1)

            def project(g, k, b):
                for mm_done, split, written, full, parts, src, bias, evac in (
                        (q_mm, q_split, q_written, qf, q_parts, 2, bq, q_evac),
                        (k_mm, k_split, k_written, kf, k_parts, 4, bk, k_evac)):
                    act.wait_ge(mm_done, g + 1)
                    act.wait_ge(split, g + 1)
                    nc.scalar.activation(full[:, k, :], bank(src + k), ACT.Identity, bias=bias[:, :])
                    act.wait_ge(written[k], (b + 1) * 16)
                    nc.scalar.activation(parts[:, k, 0, :], bank(src + k), ACT.Identity,
                                         bias=bias[:, :]).then_inc(evac, 1)

            modulate(0, 0, 0)
            with act.Fori(0, B - 1) as b:
                modulate(b * KG + 1, 1, b)
                project(b * KG, 0, b)
                modulate(b * KG + 2, 0, b + 1)
                project(b * KG + 1, 1, b)
            modulate(NG - 1, 1, B - 1)
            project(NG - 2, 0, B - 1)
            project(NG - 1, 1, B - 1)

            def evac_shift(m, s):
                act.wait_ge(nmaxT_ready, m + 1)
                nc.scalar.activation(nmaxT[:, s, :], bank(MISC)[0:NPART * QT, 0:P // 2].bitcast(BF16),
                                     ACT.Copy).then_inc(nmaxT_evac, 1)

            def evac_pv(n, s):
                act.wait_ge(pv_done, RING + QT * n)
                nc.scalar.activation(pv_sb[:, s // 2 % 2, :], bank(PV), ACT.Copy).then_inc(pv_evac, 1)

            for m in range(AHEAD - 1):
                evac_shift(m, m)

            def attention(i, first=False, last=False):
                for s in range(SLOTS):
                    n = SLOTS * i + s
                    for kt in range(QT):
                        act.wait_ge(pv_done, QT * n + kt + 1)
                        for half in range(2):
                            if kt == 1 and half == 1 and s % 2 == 0 and not (first and s == 0):
                                evac_pv(n, (s - 2) % SLOTS)
                            if kt == 3 and half == 1 and (not last or s <= SLOTS - AHEAD):
                                evac_shift(n + AHEAD - 1, (s + AHEAD - 1) % SLOTS)
                            act.wait_ge(st_ready, 16 * n + 2 * kt + half + 1)
                            nc.scalar.activation(probs[:, kt % RING, half * 512:(half + 1) * 512], bank(half),
                                                 ACT.Exp, scale=SCALE).then_inc(exp_done, 1)
                if last:
                    evac_pv(SLOTS * i + SLOTS, SLOTS - 2)

            attention(0, first=True)
            with act.Fori(1, ITERS - 1) as i:
                attention(i)
            attention(ITERS - 1, last=True)

            with act.Fori(0, B) as b:
                for k in range(KG):
                    g = b * KG + k
                    act.wait_ge(ao_ready, KG + g + 1)
                    nc.scalar.activation(oT[:, k, :], bank(k), ACT.Copy).then_inc(ao_evac, 1)
            with act.Fori(0, B) as b:
                for k in range(KG):
                    g = b * KG + k
                    act.wait_ge(x2T_ready, 2 + g + 1)
                    wait_apart(act, h2_low, (b + 1) * KG)
                    nc.scalar.activation(hT[:, k, :], bank(4 + k), ACT.Identity,
                                         bias=mod_c[:, 3, ds(b, 1)], scale=mod_c[:, 4, ds(b, 1)])
                    nc.scalar.activation(h2[:, 0, ds(g * G, G)], bank(4 + k), ACT.Identity,
                                         bias=mod_c[:, 3, ds(b, 1)], scale=mod_c[:, 4, ds(b, 1)]).then_inc(h2_ready, 1)
            act.wait_ge(w_chain, 1)
            nc.scalar.activation(wts[:, 1, :], wts[:, 0, :], ACT.Exp).then_inc(e_exp, 1)
            act.wait_ge(sel_ready, 1)
            for n in range(NT // 8):
                act.wait_ge(wpT_ready, n + 1)
                nc.scalar.activation(wT_parts[0:NPART * E, n * 8 * P:(n + 1) * 8 * P], bank(4 + n)[0:NPART * E, :].bitcast(BF16),
                                     ACT.Copy).then_inc(wpT_evac, 1)

            def experts(g, first=False):
                for e in range(E):
                    unit = g * E + e
                    for fc in range(FC):
                        n, u = e * FC + fc, (e % 2) * FC + fc
                        act.wait_ge(h_mm, g * E * FC + n + 1)
                        if fc == 0:
                            act.wait_ge(y2_mm, unit + 1)
                        if fc < FC - 1:
                            act.wait_ge(low_pool, unit * (FC - 1) + fc + 1)
                        else:
                            act.wait_ge(low_dve, unit + 1)
                        nc.scalar.activation(hid[:, fc, :], bank(n % 4), ACT.Gelu, bias=b1c[:, n:n + 1])
                        nc.scalar.activation(hid_hl[:, 0, u, :], bank(n % 4), ACT.Gelu,
                                             bias=b1c[:, n:n + 1]).then_inc(gelu_done, 1)
                    act.wait_ge(wb_mm, unit + 1)
                    act.wait_ge(y2_evac, unit + 1)
                    nc.scalar.activation(w_bc[:, e % 2, :], bank(6), ACT.Copy).then_inc(wb_evac, 1)
                    if e == 1 and not first:
                        gate(g - 1)

            def gate(g):
                wait_apart(act, y2_evac, 2 + (g + 1) * E)
                nc.scalar.activation(acc_gb[:, :], acc[:, :], ACT.Copy,
                                     scale=gb_c[:, 0, ds(g // KG, 1)]).then_inc(gated, 1)

            experts(0, first=True)
            with act.Fori(1, NG) as g:
                experts(g)
            gate(NG - 1)

        @block.vector
        def _(dve):
            dve.sem_inc(o_done, 1)
            dve.sem_inc(q_split, 2)
            dve.sem_inc(k_split, 2)
            dve.sem_inc(v_evac, 2)
            dve.sem_inc(mx_free, 2)
            dve.sem_inc(y2_evac, 2)
            dve.sem_inc(low_dve, 1)
            dve.sem_inc(out_ready, 1)
            dve.sem_inc(g_evac, 2)
            dve.sem_inc(y_scaled, 2)
            chain = [0]

            def link(ins):
                chain[0] += 1
                ins.then_inc(dve_chain, 1)
                dve.wait_ge(dve_chain, chain[0])

            for e in range(E):
                last = nc.vector.memset(iota_e[:, e:e + 1], float(e))
            def silu_and_gates():
                dve.wait_ge(c_exp_done, 1)
                link(nc.vector.tensor_scalar(silu_t[:, 1, :], silu_t[:, 0, :], 1.0, None, ALU.add))
                link(nc.vector.reciprocal(silu_t[:, 0, :], silu_t[:, 1, :]))
                link(nc.vector.tensor_tensor(siluT[:, :], cT[:, :], silu_t[:, 0, :], ALU.mult))
                for b in range(B):
                    last = nc.vector.tensor_copy(silu_b[:, b, :], siluT[:, b:b + 1].broadcast_to([P, P]))
                last.then_inc(silu_done, 1)
                dve.wait_ge(mod_done, 1)
                modp = bank(2)[:, 0:MOD * B].rearrange("p (m b) -> p m b", b=B)
                link(nc.vector.tensor_copy(mod_c[:, :, :], modp))
                for m in (1, 4):
                    last = nc.vector.tensor_scalar(mod_c[:, m, :], mod_c[:, m, :], 1.0, None, ALU.add)
                link(last)
                for src, t0, t1, dst in (
                        (bank(3), gate_t[:, 0, :, :].rearrange("p b d -> p (b d)"),
                         gate_t[:, 1, :, :].rearrange("p b d -> p (b d)"), gaB[:, :, :].rearrange("p b d -> p (b d)")),
                        (mod_c[:, 5, :], gb_c[:, 1, :], gb_c[:, 2, :], gb_c[:, 0, :])):
                    link(nc.vector.tensor_scalar(t0, src, 0.0, 2.0, ALU.is_ge, ALU.mult))
                    link(nc.vector.tensor_scalar(t1, src, -1.0, None, ALU.mult))
                    link(nc.vector.tensor_tensor(t1, src, t1, ALU.max))
                    link(nc.vector.tensor_scalar(t1, t1, 0.25, None, ALU.max))
                    link(nc.vector.scalar_tensor_tensor(dst, t0, -1.0, t1, ALU.add, ALU.mult))

            def rows(g, t):
                return x_sb[:, ds(g, 1), t, :].rearrange("p a d -> p (a d)")

            def row_stats(g):
                for t in range(GT):
                    ins = nc.vector.bn_stats(stats[:, ds(g * GT + t, 1), :].rearrange("p a n -> p (a n)"), rows(g, t))
                return ins

            def row_moments():
                m0, v0, m1, v1 = (stats[:, :, n] for n in (1, 2, 4, 5))
                link(nc.vector.tensor_tensor(mean[:, :], m0, m1, ALU.add))
                link(nc.vector.tensor_tensor(var[:, 0, :], m0, m1, ALU.subtract))
                link(nc.vector.tensor_tensor(var[:, 1, :], v0, v1, ALU.add))
                link(nc.vector.tensor_tensor(var[:, 2, :], var[:, 0, :], var[:, 0, :], ALU.mult))
                link(nc.vector.tensor_scalar(var[:, 0, :], var[:, 2, :], 0.25, None, ALU.mult))
                nc.vector.scalar_tensor_tensor(var[:, 3, :], var[:, 1, :], 1.0 / D, var[:, 0, :],
                                               ALU.mult, ALU.add).then_inc(var_ready, 1)
                link(nc.vector.tensor_scalar(mean[:, :], mean[:, :], 0.5, None, ALU.mult))

            def normalise_rows(g, k, done, transposed):
                dve.wait_ge(transposed, g + 1)
                for t in range(GT):
                    one = [a[:, ds(g * GT + t, 1)] for a in (mean, rstd)]
                    ins = nc.vector.tensor_scalar(xn[:, k, t, :], rows(g, t), one[0], one[1], ALU.subtract, ALU.mult)
                ins.then_inc(done, 1)

            silu_and_gates()
            for half in range(2):
                dve.wait_ge(x_loaded[half], 16)
                with dve.Fori(half * NG // 2, (half + 1) * NG // 2) as g:
                    row_stats(g).then_inc(stats_done, 1)
            dve.wait_ge(stats_done, NG)
            row_moments()
            dve.wait_ge(w_loaded, W_LOADS * 16)
            for b in range(B):
                last = nc.vector.tensor_tensor(gaboB[:, b, :], gaB[:, b, :], boB[:, :], ALU.mult)
            nc.vector.reciprocal(rtemp[:, :], tempB[:, :]).then_inc(mod_ready, 1)
            dve.wait_ge(rstd_ready, 1)
            HQ = H * QT * DK

            def split_qv(g, k, b):
                dve.wait_ge(v_mm, g + 1)
                v_v = v_all[:, ds(b * HQ, HQ)].rearrange("p (h k d) -> p k h d", h=H, k=QT)
                for t in range(GT):
                    ins = nc.vector.tensor_tensor(
                        v_v[:, k * GT + t, :, :],
                        bank(6 + k)[:, t * D:(t + 1) * D].rearrange("p (h d) -> p h d", h=H),
                        bvB[:, :].rearrange("p (h d) -> p h d", h=H), ALU.add)
                ins.then_inc(v_evac, 1)
                dve.wait_ge(q_evac, 2 + g + 1)
                dve.wait_ge(q_written[k], (b + 1) * 16)
                part = [q_parts[:, k, n, :] for n in range(NPART)]
                nc.vector.tensor_tensor(qf[:, k, :], qf[:, k, :], part[0], ALU.subtract).then_inc(qs_chain, 1)
                dve.wait_ge(qs_chain, g * 2 + 1)
                nc.vector.tensor_copy(part[1], qf[:, k, :]).then_inc(qs_chain, 1)
                dve.wait_ge(qs_chain, g * 2 + 2)
                nc.vector.tensor_tensor(part[2], qf[:, k, :], part[1], ALU.subtract).then_inc(q_split, 1)

            def qkv_rows(g, k):
                normalise_rows(g, k, xn_ready, xT_ready)

            qkv_rows(0, 0)
            qkv_rows(1, 1)
            dve.wait_ge(rstd_ready, 2)
            with dve.Fori(0, B - 1) as b:
                for k in range(KG):
                    qkv_rows(b * KG + k + 2, k)
                    split_qv(b * KG + k, k, b)
            split_qv(NG - 2, 0, B - 1)
            split_qv(NG - 1, 1, B - 1)

            def reduce_max(m, s, qt):
                dve.wait_ge(mx_ready, QT * m + qt + 1)
                nc.vector.tensor_reduce(nmax[:, s, qt:qt + 1], bank(2 + 2 * (qt % 2), 2), AX.X, ALU.max,
                                        negate=True).then_inc(mx_free, 1)

            def row_sums(m, s):
                dve.wait_ge(oT_ready, m + 1)
                o_ps = bank(MISC)[:, 0:GT * 4 * HW].rearrange("p (x e) -> p x e", e=HW)
                nc.vector.reciprocal(rsum[:, s // 2 % 2, :], o_ps[:, :, DK]).then_inc(rsum_ready, 1)

            def normalise(m, s):
                dve.wait_ge(rsum_ready, m + 1)
                o_ps = bank(MISC)[:, 0:GT * 4 * HW].rearrange("p (x e) -> p x e", e=HW)
                nc.vector.tensor_tensor(
                    o_all[:, ds(m, 1), :, :, :].rearrange("p o t k (a d) -> p (o t k a) d", a=2),
                    o_ps[:, :, 0:DK],
                    rsum[:, s // 2 % 2, :].rearrange("p (x a) -> p x a", a=1).broadcast_to([P, 4 * GT, DK]),
                    ALU.mult).then_inc(o_done, 1)

            for m in range(AHEAD):
                for qt in range(QT):
                    reduce_max(m, m, qt)

            def attention(i, first=False, last=False):
                for s in range(SLOTS):
                    for kt in range(QT):
                        if not last or s < SLOTS - AHEAD:
                            reduce_max(SLOTS * i + s + AHEAD, (s + AHEAD) % SLOTS, kt)
                        if s % 2 == 0 and not (first and s == 0):
                            m = SLOTS // 2 * i + s // 2 - 1
                            if kt == 4:
                                row_sums(m, (s - 2) % SLOTS)
                            if kt == 5:
                                normalise(m, (s - 2) % SLOTS)
                if last:
                    row_sums(OUTS - 1, SLOTS - 2)
                    normalise(OUTS - 1, SLOTS - 2)

            attention(0, first=True)
            with dve.Fori(1, ITERS - 1) as i:
                attention(i)
            attention(ITERS - 1, last=True)

            with dve.Fori(0, B) as b:
                for k in range(KG):
                    g = b * KG + k
                    dve.wait_ge(y_mm, g + 1)
                    for t in range(GT):
                        last = nc.vector.tensor_tensor(y_sb[:, k, t, :], bank(2 + k)[:, t * D:(t + 1) * D],
                                                       gaB[:, ds(b, 1), :].rearrange("p a d -> p (a d)"), ALU.mult)
                    last.then_inc(y_scaled, 1)
                    dve.wait_ge(y_scaled, 2 + g + 1)
                    dve.wait_ge(xg_ready, g + 1)
                    xg = x_sb[:, ds(g, 1), :, :].rearrange("p a t d -> p (a t d)")
                    nc.vector.tensor_tensor(xg, y_sb[:, k, :, :].rearrange("p t d -> p (t d)"), xg,
                                            ALU.add).then_inc(x2_ready, 1)
                    wait_apart(dve, x2_ready, g + 1)
                    row_stats(g).then_inc(stats_done, 1)
            dve.wait_ge(stats_done, 2 * NG)
            row_moments()
            dve.wait_ge(rstd_ready, 3)

            def h2_rows(g, k):
                normalise_rows(g, k, xn2_ready, x2T_ready)

            def router(g, k):
                dve.wait_ge(g_mm, g + 1)
                nc.vector.tensor_tensor(logits[:, ds(g * GT, GT), :],
                                        bank(6 + k)[:, 0:GT * E].rearrange("p (t e) -> p t e", e=E),
                                        gbiasB[:, :].rearrange("p (a e) -> p a e", a=1).broadcast_to([P, GT, E]),
                                        ALU.add).then_inc(g_evac, 1)

            h2_rows(0, 0)
            h2_rows(1, 1)
            dve.wait_ge(rstd_ready, 4)
            with dve.Fori(0, B - 1) as b:
                for k in range(KG):
                    h2_rows(b * KG + k + 2, k)
                    router(b * KG + k, k)
            router(NG - 2, 0)
            router(NG - 1, 1)
            dve.wait_ge(g_evac, 2 + NG)
            lg = logits[:, :, :].rearrange("p t e -> p (t e)")
            link(nc.vector.tensor_scalar(lg, lg, rtemp[:, :], None, ALU.mult))
            for t in range(NT):
                last = nc.vector.max(eight_v[:, t, :], logits[:, t, :])
            link(last)
            for t in range(NT):
                last = nc.vector.max_index(eight_i[:, t, :], eight_v[:, t, :], logits[:, t, :])
            link(last)
            for n in range(2):
                last = nc.vector.tensor_copy(top_if[:, n, :], eight_i[:, :, n])
            link(last)
            nc.vector.tensor_tensor(wts[:, 0, :], eight_v[:, :, 1], eight_v[:, :, 0], ALU.subtract).then_inc(w_chain, 1)
            dve.wait_ge(e_exp, 1)
            link(nc.vector.tensor_scalar(wts[:, 2, :], wts[:, 1, :], 1.0, None, ALU.add))
            link(nc.vector.reciprocal(wts[:, 3, :], wts[:, 2, :]))
            link(nc.vector.tensor_tensor(wts[:, 2, :], wts[:, 1, :], wts[:, 3, :], ALU.mult))
            def each(a):
                return a.rearrange("p (t a) -> p t a", a=1).broadcast_to([P, NT, E])

            experts_of = iota_e[:, :].rearrange("p (a e) -> p a e", a=1).broadcast_to([P, NT, E])
            for n in range(2):
                last = nc.vector.tensor_tensor(hot[:, n, :, :], experts_of, each(top_if[:, n, :]), ALU.is_equal)
            link(last)
            for n, w in ((0, 3), (1, 2)):
                last = nc.vector.tensor_tensor(hot[:, n, :, :], hot[:, n, :, :], each(wts[:, w, :]), ALU.mult)
            link(last)
            flat = [a.rearrange("p t e -> p (t e)") for a in (w_exp[:, :, :], hot[:, 0, :, :], hot[:, 1, :, :])]
            link(nc.vector.tensor_tensor(flat[0], flat[1], flat[2], ALU.add))
            rest = [w_exp[:, :, :], w_rest[:, 0, :, :], w_rest[:, 1, :, :]]
            for n in range(NPART):
                ins = nc.vector.tensor_copy(w_parts[:, :, n, :], rest[n])
                if n < NPART - 1:
                    link(ins)
                    link(nc.vector.tensor_tensor(rest[n + 1], rest[n], w_parts[:, :, n, :], ALU.subtract))
            ins.then_inc(wp_ready, 1)

            def combine(g, e):
                unit = g * E + e
                dve.wait_ge(y2_mm, 2 + unit + 1)
                dve.wait_ge(wb_evac, 1 + unit + 1)
                if e == 0:
                    dve.wait_ge(gated, g + 1)
                    nc.vector.scalar_tensor_tensor(acc[:, :], bank(4 + e % 2), b2c[:, e:e + 1], w_bc[:, e % 2, :],
                                                   ALU.add, ALU.mult).then_inc(y2_evac, 1)
                else:
                    nc.vector.scalar_tensor_tensor(acc_t[:, :], bank(4 + e % 2), b2c[:, e:e + 1], w_bc[:, e % 2, :],
                                                   ALU.add, ALU.mult).then_inc(acc_chain, 1)
                    dve.wait_ge(acc_chain, g * (E - 1) + e)
                    dve.wait_ge(y2_evac, 2 + unit)
                    nc.vector.tensor_tensor(acc[:, :], acc[:, :], acc_t[:, :], ALU.add).then_inc(y2_evac, 1)

            def finish(g):
                dve.wait_ge(outT_mm, g + 1)
                dve.wait_ge(out_stored, (g + 1) * 16)
                nc.vector.tensor_tensor(out_sb[:, :, :].rearrange("p t d -> p (t d)"), bank(7),
                                        x_sb[:, ds(g, 1), :, :].rearrange("p a t d -> p (a t d)"),
                                        ALU.add).then_inc(out_ready, 1)

            def experts(g, first=False):
                for e in range(E):
                    unit = g * E + e
                    if not (first and e == 0):
                        combine(g if e else g - 1, (e - 1) % E)
                    dve.wait_ge(gelu_done, 4 + (unit + 1) * FC)
                    u = (e % 2) * FC + FC - 1
                    nc.vector.tensor_tensor(hid_hl[:, 1, u, :], hid[:, FC - 1, :], hid_hl[:, 0, u, :].bitcast(F32),
                                            ALU.subtract).then_inc(low_dve, 1)
                    if e == 3 and not first:
                        finish(g - 1)

            experts(0, first=True)
            with dve.Fori(1, NG) as g:
                experts(g)
            combine(NG - 1, E - 1)
            finish(NG - 1)

        @block.tensor
        def _(pe):
            mm = nc.tensor.matmul
            pe.sem_inc(pv_done, RING)
            pe.sem_inc(y2_mm, 2)
            pe.sem_inc(ao_ready, KG)
            pe.sem_inc(xT_ready, 2)
            pe.sem_inc(x2T_ready, 2)
            pe.wait_ge(silu_done, 1)
            for m in range(MOD):
                mm(bank(2)[:, m * B:(m + 1) * B], wmod[:, m * D:(m + 1) * D], siluT[:, :], start=True, stop=True)
            for b in range(B):
                last = mm(bank(3)[:, b * D:(b + 1) * D], silu_b[:, b, :], wmod[:, 2 * D:3 * D], start=True, stop=True)
            last.then_inc(mod_done, 1)
            pe.wait_ge(ident_made, 2)
            pe.wait_ge(w_loaded, W_LOADS * 16)
            for n in range(4):
                nc.tensor.transpose(bank(0)[:, n * D:(n + 1) * D], w_raw[:, n, :], ident[:, :])
            nc.tensor.transpose(bank(1)[:, 0:E * FC], b1_raw[:, :], ident[0:E * FC, 0:E * FC])
            nc.tensor.transpose(bank(1)[:, E * FC:E * FC + E], b2_raw[:, :], ident[0:E, 0:E]).then_inc(w_transposed, 1)
            pe.wait_ge(wT_ready, 3)
            pe.wait_ge(mod_ready, 1)

            def transpose_rows(g, k, base, ready, read, done):
                pe.wait_ge(ready, g + 1)
                pe.wait_ge(read, g + 1)
                for t in range(GT):
                    ins = nc.tensor.transpose(bank(base + k)[:, t * P:(t + 1) * P], xn[:, k, t, :], ident[:, :])
                ins.then_inc(done, 1)

            def qkv(g, k):
                pe.wait_ge(hT_ready, 2 + g + 1)
                pe.wait_ge(q_evac, g + 1)
                mm(bank(2 + k), wT[:, 0, :], hT[:, k, :], start=True, stop=True).then_inc(q_mm, 1)
                pe.wait_ge(k_evac, g + 1)
                mm(bank(4 + k), wT[:, 1, :], hT[:, k, :], start=True, stop=True).then_inc(k_mm, 1)
                pe.wait_ge(v_evac, g + 1)
                for t in range(GT):
                    ins = mm(bank(6 + k)[:, t * D:(t + 1) * D], hT[:, k, t * P:(t + 1) * P], wT[:, 2, :],
                             start=True, stop=True)
                ins.then_inc(v_mm, 1)

            def x_rows(g, k):
                transpose_rows(g, k, 0, xn_ready, hT_ready, xT_ready)

            x_rows(0, 0)
            with pe.Fori(0, B - 1) as b:
                x_rows(b * KG + 1, 1)
                qkv(b * KG, 0)
                x_rows(b * KG + 2, 0)
                qkv(b * KG + 1, 1)
            x_rows(NG - 1, 1)
            qkv(NG - 2, 0)
            qkv(NG - 1, 1)
            pe.wait_ge(q_evac, 2 + NG)
            pe.wait_ge(k_evac, 2 + NG)
            pe.wait_ge(v_evac, 2 + NG)

            def scores_for_max(i, s, m, qt, halves=(0, 1)):
                if qt == 0 and 0 in halves:
                    pe.wait_ge(q_loaded[s], 3 * 16 * (i + 1))
                    pe.wait_ge(k_loaded[s // 2], 2 * 3 * 16 * (i + 1))
                if 0 in halves:
                    pe.wait_ge(mx_free, QT * m + qt + 1)
                for half in halves:
                    last = mm(bank(2 + 2 * (qt % 2) + half), q_stack[0:SHIFT, s, qt * P:(qt + 1) * P],
                              k_stack[0:SHIFT, s // 2, half * 512:(half + 1) * 512], start=True, stop=True)
                if 1 in halves:
                    last.then_inc(mx_ready, 1)

            def scores(i, s, kt, half):
                n = SLOTS * i + s
                if kt == 0 and half == 0:
                    pe.wait_ge(shift_loaded[s], 16 * (i + 1))
                pe.wait_ge(exp_done, 16 * n + 2 * kt + half + 1)
                mm(bank(half), k_stack[0:KROWS, s // 2, kt * P:(kt + 1) * P],
                   q_stack[0:KROWS, s, half * 512:(half + 1) * 512], start=True, stop=True).then_inc(st_ready, 1)

            def transpose_shift(m, s, o_count):
                pe.wait_ge(nmax_split, m + 1)
                pe.wait_ge(o_done, 1 + o_count)
                pe.wait_ge(nmaxT_evac, 1 + m)
                nc.tensor.transpose(bank(MISC)[0:NPART * QT, 0:P // 2].bitcast(BF16),
                                    nmax_p[:, s, :, :].rearrange("p n t -> p (n t)"), ident_b[:, :])\
                  .then_inc(nmaxT_ready, 1)

            def transpose_out(m, s, shift_count):
                pe.wait_ge(pv_evac, 1 + m + 1)
                pe.wait_ge(nmaxT_evac, 1 + shift_count)
                pe.wait_ge(o_done, 1 + m)
                for t in range(GT):
                    last = mm(bank(MISC)[:, t * 4 * HW:(t + 1) * 4 * HW], pv_sb[:, s // 2 % 2, t * P:(t + 1) * P],
                              to_rows[:, :, :].rearrange("p h e -> p (h e)"), start=True, stop=True)
                last.then_inc(oT_ready, 1)

            def pv(i, s, kt):
                n = SLOTS * i + s
                pe.wait_ge(exp_done, 2 + 16 * n + 2 * kt + 4)
                if kt == 0:
                    if s % 2 == 0:
                        pe.wait_ge(pv_evac, 1 + SLOTS // 2 * i + s // 2)
                    if s % QUAD == 0:
                        pe.wait_ge(v_staged, 2 * i + s // QUAD + 1)
                for c in range(2):
                    for h in range(2):
                        j = 2 * c + h
                        last = mm(bank(PV)[32 * j:32 * j + 32, :], v_stage[:, s, kt + c, :],
                                  probs[:, (kt + c) % RING, h * 512:(h + 1) * 512], start=kt == 0 and s % 2 == 0, stop=kt == QT - 2 and s % 2 == 1)
                last.then_inc(pv_done, 2)

            pe.wait_ge(stacks_cleared, 3)
            for m in range(AHEAD):
                for qt in range(QT):
                    scores_for_max(0, m, m, qt)
                if m:
                    transpose_shift(m - 1, m - 1, 0)

            def attention(i, first=False, last=False):
                for s in range(SLOTS):
                    n = SLOTS * i + s

                    def ahead(qt, *halves):
                        if not last or s < SLOTS - AHEAD:
                            scores_for_max(i + (s + AHEAD) // SLOTS, (s + AHEAD) % SLOTS, n + AHEAD, qt, halves)

                    for kt in range(0, QT, 2):
                        scores(i, s, kt, 0)
                        ahead(kt, 0, 1)
                        ahead(kt + 1, 0)
                        scores(i, s, kt, 1)
                        ahead(kt + 1, 1)
                        scores(i, s, kt + 1, 0)
                        if kt == 2 and (not last or s <= SLOTS - AHEAD):
                            outs = SLOTS // 2 * i + (s - 1) // 2
                            transpose_shift(n + AHEAD - 1, (s + AHEAD - 1) % SLOTS, 0 if first and s == 0 else outs)
                        if kt:
                            pv(i, s, kt - 2)
                        elif not (first and s == 0):
                            pv(i if s else i - 1, (s - 1) % SLOTS, QT - 2)
                        scores(i, s, kt + 1, 1)
                        if kt == 2 and s % 2 == 0 and not (first and s == 0):
                            transpose_out(SLOTS // 2 * i + s // 2 - 1, (s - 2) % SLOTS,
                                          min(n + AHEAD, B * H) if last else n + AHEAD)
                if last:
                    pv(i, SLOTS - 1, QT - 2)
                    transpose_out(OUTS - 1, SLOTS - 2, B * H)

            attention(0, first=True)
            with pe.Fori(1, ITERS - 1) as i:
                attention(i)
            attention(ITERS - 1, last=True)
            pe.wait_ge(o_done, 1 + OUTS)

            with pe.Fori(0, B) as b:
                for k in range(KG):
                    g = b * KG + k
                    pe.wait_ge(o_staged, g + 1)
                    pe.wait_ge(ao_evac, g + 1)
                    for t in range(GT):
                        last = nc.tensor.transpose(bank(k)[:, t * P:(t + 1) * P], o_st[:, k, t * D:(t + 1) * D],
                                                   ident[:, :])
                    last.then_inc(ao_ready, 1)
                    pe.wait_ge(ao_evac, 2 + g + 1)
                    pe.wait_ge(y_scaled, g + 1)
                    for t in range(GT):
                        last = mm(bank(2 + k)[:, t * D:(t + 1) * D], oT[:, k, t * P:(t + 1) * P], wT[:, 3, :],
                                  start=True, stop=True)
                    last.then_inc(y_mm, 1)

            def h2_rows(g, k):
                transpose_rows(g, k, 4, xn2_ready, h2_ready, x2T_ready)

            def router(g, k):
                pe.wait_ge(h2_ready, 2 + g + 1)
                pe.wait_ge(g_evac, g + 1)
                for t in range(GT):
                    ins = mm(bank(6 + k)[:, t * E:(t + 1) * E], hT[:, k, t * P:(t + 1) * P], gate_w[:, :],
                             start=True, stop=True)
                ins.then_inc(g_mm, 1)

            h2_rows(0, 0)
            with pe.Fori(0, B - 1) as b:
                h2_rows(b * KG + 1, 1)
                router(b * KG, 0)
                h2_rows(b * KG + 2, 0)
                router(b * KG + 1, 1)
            h2_rows(NG - 1, 1)
            router(NG - 2, 0)
            router(NG - 1, 1)
            pe.wait_ge(g_evac, 2 + NG)
            pe.wait_ge(h2_low, KG + NG)
            pe.wait_ge(w_split, 1 + E)
            pe.wait_ge(wp_ready, 1)
            for n in range(NT):
                ins = nc.tensor.transpose(
                    bank(4 + n // 8)[0:NPART * E, (n % 8) * P // 2:(n % 8 + 1) * P // 2].bitcast(BF16),
                    w_parts[:, n, :, :].rearrange("p n e -> p (n e)"), ident_b[:, :])
                if n % 8 == 7:
                    ins.then_inc(wpT_ready, 1)
            pe.wait_ge(wpT_evac, NT // 8)
            pe.wait_ge(sel_ready, 1)

            PASSES = ((0, 0), (1, 0), (0, 1))

            def up(g, e):
                unit = g * E + e
                for fc in range(FC):
                    n = e * FC + fc
                    pe.wait_ge(gelu_done, g * E * FC + n + 1)
                    for j, (a, b) in enumerate(PASSES):
                        ins = mm(bank(n % 4), w1[:, a, e, fc * P:(fc + 1) * P], h2[:, b, ds(g * G, G)],
                                 start=j == 0, stop=j == 2)
                    ins.then_inc(h_mm, 1)
                pe.wait_ge(wb_evac, unit + 1)
                mm(bank(6), sel[:, e, :], wT_parts[:, ds(g * G, G)], start=True, stop=True).then_inc(wb_mm, 1)

            def down(g, e):
                unit = g * E + e
                pe.wait_ge(y2_evac, unit + 1)
                for fc in range(FC):
                    pe.wait_ge(gelu_done, 4 + unit * FC + fc + 1)
                    if fc < FC - 1:
                        pe.wait_ge(low_pool, (FC - 1) * (unit + 1) + fc + 1)
                    else:
                        pe.wait_ge(low_dve, 1 + unit + 1)
                    for j, (a, b) in enumerate(PASSES):
                        ins = mm(bank(4 + e % 2), w2[:, a, e, fc * P:(fc + 1) * P],
                                 hid_hl[:, b, (e % 2) * FC + fc, :], start=fc + j == 0, stop=fc == FC - 1 and j == 2)
                ins.then_inc(y2_mm, 1)

            def rows_again(g):
                pe.wait_ge(gated, 1 + g + 1)
                pe.wait_ge(out_ready, g + 1)
                for t in range(GT):
                    ins = nc.tensor.transpose(bank(7)[:, t * P:(t + 1) * P], acc_gb[:, t * P:(t + 1) * P], ident[:, :])
                ins.then_inc(outT_mm, 1)

            def experts(g, first=False):
                for e in range(E):
                    up(g, e)
                    if not (first and e == 0):
                        down(g if e else g - 1, (e - 1) % E)
                    if e == 2 and not first:
                        rows_again(g - 1)

            experts(0, first=True)
            with pe.Fori(1, NG) as g:
                experts(g)
            down(NG - 1, E - 1)
            rows_again(NG - 1)


_INS = ["L0_attn_x", "L0_attn_Wq", "L0_attn_bq", "L0_attn_Wk", "L0_attn_bk", "L0_attn_Wv", "L0_attn_bv",
        "L0_attn_Wo", "L0_attn_bo", "L0_ffn_W1", "L0_ffn_b1", "L0_ffn_W2", "L0_ffn_b2", "L0_ffn_gate_w",
        "L0_ffn_gate_b", "L0_ffn_temperature", "L0_c", "L0_wmod"]


def kernel(**inputs):
    import numpy as _np
    import concourse.bacc as _bacc
    from concourse import mybir as _mybir
    from concourse.bass_utils import run_bass_kernel_spmd as _run

    nc = _bacc.Bacc("TRN2", target_bir_lowering=False, num_devices=1)
    arrays, args = {}, []
    for name in _INS:
        a = _np.ascontiguousarray(inputs[name])
        if name == "L0_ffn_temperature":
            a = a.reshape(1)
        arrays[f"in_{name}"] = a
        args.append(nc.dram_tensor(f"in_{name}", a.shape, _mybir.dt.from_np(a.dtype), kind="ExternalInput").ap())
    shape = inputs["L0_attn_x"].shape
    out = nc.dram_tensor("out_0", shape, _mybir.dt.float32, kind="ExternalOutput").ap()
    adaln_block(nc, *args, out)
    r = _run(nc, [arrays], core_ids=[0])
    return r.results[0]["out_0"]
```

```python
from contextlib import ExitStack

import concourse.bass as bass
import numpy as np
from concourse import mybir


def adaln_block(nc, x_d, wq_d, bq_d, wk_d, bk_d, wv_d, bv_d, wo_d, bo_d,
                w1_d, b1_d, w2_d, b2_d, gw_d, gb_d, temp_d, c_d, wmod_d, out_d):
    F32, BF16, U32, F32R = mybir.dt.float32, mybir.dt.bfloat16, mybir.dt.uint32, mybir.dt.float32r
    ALU, ACT, AX = mybir.AluOpType, mybir.ActivationFunctionType, mybir.AxisListType
    ds = bass.ds

    P = 128
    B, S, D = x_d.shape
    E, _, F = w1_d.shape
    H, DK = 16, D // 16
    MOD = 6
    G = 512
    GT = G // P
    KG = S // G
    NG = B * KG
    QT = S // P
    FC = F // P
    SLOTS = 8
    ITERS = B * H // SLOTS
    AHEAD = 2
    QUAD = 4
    NPART = 3
    LATE = (NG - KG) * GT
    PAIRS = 6
    ROWS = PAIRS * DK
    SHIFT = 2 * ROWS
    NT = B * QT
    KROWS = SHIFT + NPART
    HW = 16
    OUTS = B * H // 2
    RING = 4
    WRING = 4
    PV, MISC = 6, 7
    W_LOADS = 13
    SCALE = 1.0 / float(np.sqrt(DK))
    EPS = 1e-5

    ctx = ExitStack()
    with ctx:
        def sb(name, shape, dt=F32):
            return ctx.enter_context(nc.sbuf_tensor(name, shape, dt))

        def sem(name):
            return ctx.enter_context(nc.semaphore(name))

        x_sb = sb("x_sb", [P, NG, GT, D])
        w1 = sb("w1", [P, 2, E, F], F32R)
        w2 = sb("w2", [P, 2, E, FC * D], F32R)
        wT = sb("wT", [P, 4, D])
        ident = sb("ident", [P, P])
        ident_b = sb("ident_b", [P, P], BF16)
        cT = sb("cT", [P, B])
        silu_t = sb("silu_t", [P, 2, B])
        siluT = sb("siluT", [P, B])
        mod_c = sb("mod_c", [P, MOD, B])
        wo_ga = sb("wo_ga", [P, B, D])
        gaboB = sb("gaboB", [P, B, D])
        gbiasB = sb("gbiasB", [P, E])
        tempB = sb("tempB", [P, 1])
        rtemp = sb("rtemp", [P, 1])
        b1c = sb("b1c", [P, E * FC])
        bq = sb("bq", [P, 1])
        bk = sb("bk", [P, 1])
        gate_w = sb("gate_w", [P, E])
        mhalf = sb("mhalf", [P, NT])
        to_rows = sb("to_rows", [P, 2, 2 * HW])
        stats = sb("stats", [P, NT, 6])
        mean = sb("mean", [P, NT])
        var = sb("var", [P, 4, NT])
        vareps = sb("vareps", [P, NT])
        rstd = sb("rstd", [P, NT])
        xn = sb("xn", [P, KG, GT, D])
        hT = sb("hT", [P, KG, G])
        qf = sb("qf", [P, KG, G])
        kf = sb("kf", [P, KG, G])
        o_st = qf
        oT = kf
        iota_e = sb("iota_e", [P, E])
        b2c = sb("b2c", [P, E])
        gb_c = sb("gb_c", [P, 3, B])

        def placed_in(stack):
            return lambda name, shape, dt=F32: stack.enter_context(nc.sbuf_tensor(name, shape, dt))

        with ExitStack() as attention_phase:
            sa = placed_in(attention_phase)
            o_all = sa("o_all", [P, OUTS + 1, KG, GT, 2 * DK])
            v_all = sa("v_all", [P, B * H * QT * DK])
            q_stack = sa("q_stack", [P, SLOTS, S], BF16)
            k_stack = sa("k_stack", [P, SLOTS // 2, S], BF16)
            v_stage = sa("v_stage", [P, SLOTS, QT, 32])
            rsum = sa("rsum", [P, 2, 4 * QT // 2])
            nmax = sa("nmax", [P, SLOTS, QT])
            nmax_r = sa("nmax_r", [P, SLOTS, 2, QT])
            nmax_p = sa("nmax_p", [P, SLOTS, NPART, QT], BF16)
            nmaxT = sa("nmaxT", [NPART * QT, SLOTS, P], BF16)
            with ExitStack() as start_phase:
                ss = placed_in(start_phase)
                w_raw = ss("w_raw", [P, 4, D])
                wmod = ss("wmod", [P, MOD * D])
                silu_b = ss("silu_b", [P, B, P])
                gaB = ss("gaB", [P, B, D])
                gate_t = ss("gate_t", [P, 2, B, D])
                q_parts = ss("q_parts", [P, KG, NPART, G], BF16)
                k_parts = ss("k_parts", [P, KG, NPART, G], BF16)
                bvB = ss("bvB", [P, D])
                boB = ss("boB", [P, D])
                b2_raw = ss("b2_raw", [E, D])
                b1_raw = ss("b1_raw", [E * FC, P])
            probs = sa("probs", [P, RING, S])
            w12_raw = sa("w12_raw", [P, 2, F])
            pv_sb = sa("pv_sb", [P, 2, G])
        with ExitStack() as ffn_phase:
            sf = placed_in(ffn_phase)
            h2 = sf("h2", [P, 2, NG * G], F32R)
            w_exp = sf("w_exp", [P, NG * GT, E])
            w_rows = sf("w_rows", [P, 2, P])
            wts = sf("wts", [P, 4, NG * GT])
            top_if = sf("top_if", [P, 2, NG * GT])
            hid = sf("hid", [P, FC, G])
            hid_hl = sf("hid_hl", [P, 2, 2 * FC, G], F32R)
            with ExitStack() as routing_phase:
                sr = placed_in(routing_phase)
                hot = sr("hot", [P, 2, NG * GT, E])
                eight_v = sr("eight_v", [P, NT, 8])
                eight_i = sr("eight_i", [P, NT, 8], U32)
                logits = sr("logits", [P, NT, E])
            acc = sf("acc", [P, G])
            acc_t = sf("acc_t", [P, G])
            acc_gb = sf("acc_gb", [P, G])
            w_bc = sf("w_bc", [P, WRING, G])
            out_sb = sf("out_sb", [P, GT, D])

        psum = ctx.enter_context(nc.psum_tensor("psum", [P, 8 * 512], F32))

        def bank(n, k=1):
            return psum[:, n * 512:(n + k) * 512]

        def st_bank(kt, half, alone):
            return bank(2 * (kt % 2) + half if alone else half)

        q_dram = nc.dram_tensor("q_dram", (B * H, DK, NPART, S), BF16, kind="Internal").ap()
        w_dram = nc.dram_tensor("w_dram", (E, NT, P), F32, kind="Internal").ap()
        k_dram = nc.dram_tensor("k_dram", (B * H, DK, NPART, S), BF16, kind="Internal").ap()

        x_loaded = [sem(f"x_loaded{half}") for half in range(2)]
        small_loaded, w_loaded = sem("small_loaded"), sem("w_loaded")
        consts_made, ident_made, stacks_cleared = sem("consts_made"), sem("ident_made"), sem("stacks_cleared")
        pool_chain, dve_chain = sem("pool_chain"), sem("dve_chain")
        c_exp_done, silu_done, mod_done, mod_ready, wo_ready, w_transposed, wT_ready = (
            sem(n) for n in ("c_exp_done", "silu_done", "mod_done", "mod_ready", "wo_ready", "w_transposed", "wT_ready"))
        stats_done, var_ready, rstd_ready, xn_ready, xT_ready, hT_ready = (
            sem(n) for n in ("stats_done", "var_ready", "rstd_ready", "xn_ready", "xT_ready", "hT_ready"))
        q_mm, k_mm, v_mm, q_evac, k_evac, v_evac, q_split, k_split = (
            sem(n) for n in ("q_mm", "k_mm", "v_mm", "q_evac", "k_evac", "v_evac", "q_split", "k_split"))
        q_written = [sem(f"q_written{k}") for k in range(KG)]
        k_written = [sem(f"k_written{k}") for k in range(KG)]
        q_loaded = [sem(f"q_loaded{s}") for s in range(SLOTS)]
        k_loaded = [sem(f"k_loaded{s}") for s in range(SLOTS // 2)]
        shift_loaded = [sem(f"shift_loaded{s}") for s in range(SLOTS)]
        st_ready, exp_done, mx_ready, mx_free, k_chain, k_second, nmax_split, nmaxT_ready, nmaxT_evac = (
            sem(n) for n in ("st_ready", "exp_done", "mx_ready", "mx_free", "k_chain", "k_second", "nmax_split", "nmaxT_ready", "nmaxT_evac"))
        pv_done, pv_evac, oT_ready, rsum_ready, o_done, v_staged = (
            sem(n) for n in ("pv_done", "pv_evac", "oT_ready", "rsum_ready", "o_done", "v_staged"))
        o_staged, xg_ready, ao_ready, ao_evac, y_mm, x2_ready = (
            sem(n) for n in ("o_staged", "xg_ready", "ao_ready", "ao_evac", "y_mm", "x2_ready"))
        xn2_ready, x2T_ready, h2_ready, g_mm, g_evac = (
            sem(n) for n in ("xn2_ready", "x2T_ready", "h2_ready", "g_mm", "g_evac"))
        logit_gap, gap_exp = sem("logit_gap"), sem("gap_exp")
        h_mm, gelu_done, y2_mm, y2_evac, acc_chain, out_ready = (
            sem(n) for n in ("h_mm", "gelu_done", "y2_mm", "y2_evac", "acc_chain", "out_ready"))
        out_stored, w12_loaded, w_split, h2_low = sem("out_stored"), sem("w12_loaded"), sem("w_split"), sem("h2_low")
        w_ready, w_rows_mm, w_rows_ready, w_written, low_pool, low_dve, gated, outT_mm = (
            sem(n) for n in ("w_ready", "w_rows_mm", "w_rows_ready", "w_written", "low_pool", "low_dve", "gated", "outT_mm"))
        w_spread = [sem(f"w_spread{n}") for n in range(WRING)]
        ws_chain = sem("ws_chain")
        q_chain, max_chain = sem("q_chain"), sem("max_chain")

        waits_apart = sem("waits_apart")

        def wait_apart(eng, semaphore, value):
            eng.wait_ge(semaphore, value)
            eng.sem_inc(waits_apart, 1)

        block = ctx.enter_context(nc.Block())
        x_v = x_d.rearrange("b s d -> (b s) d").rearrange("(g p t) d -> g p t d", p=P, t=GT)
        out_v = out_d.rearrange("b s d -> (b s) d").rearrange("(g p t) d -> g p t d", p=P, t=GT)

        @block.sync
        def _(sp):
            sp.sem_inc(out_stored, 16)
            for k in range(KG):
                sp.sem_inc(q_written[k], 16)
                sp.sem_inc(k_written[k], 16)
            sp.dma_start(cT[:, :], c_d.rearrange("b d -> d b"), allow_slow_non_contiguous=True).then_inc(small_loaded, 16)
            sp.dma_start(wmod[:, :], wmod_d).then_inc(small_loaded, 16)
            for half in range(2):
                part = slice(half * NG // 2, (half + 1) * NG // 2)
                sp.dma_start(x_sb[:, part, :, :], x_v[part].rearrange("g p t d -> p g (t d)"))\
                  .then_inc(x_loaded[half], 16)
            for n, w in enumerate((wq_d, wk_d, wv_d, wo_d)):
                sp.dma_start(w_raw[:, n, :], w).then_inc(w_loaded, 16)
            for dst, src in ((bq, bq_d), (bk, bk_d)):
                sp.dma_start(dst[:, :], src.rearrange("(d a) -> d a", a=1), allow_slow_non_contiguous=True).then_inc(w_loaded, 16)
            for dst, src in ((bvB[:, :], bv_d), (boB[:, :], bo_d), (gbiasB[:, :], gb_d)):
                sp.dma_start(dst, src.partition_broadcast(P)).then_inc(w_loaded, 16)
            sp.dma_start(tempB[:, :], temp_d.partition_broadcast(P)).then_inc(w_loaded, 16)
            sp.dma_start(gate_w[:, :], gw_d).then_inc(w_loaded, 16)
            sp.dma_start(b1_raw[:, :], b1_d.rearrange("e (c f) -> (e c) f", f=P)).then_inc(w_loaded, 16)
            sp.dma_start(b2_raw[:, :], b2_d).then_inc(w_loaded, 16)
            def store_parts(g):
                b, k = g // KG, g % KG
                for split, parts, dram, written in ((q_split, q_parts, q_dram, q_written),
                                                    (k_split, k_parts, k_dram, k_written)):
                    sp.wait_ge(split, 2 + g + 1)
                    rows = dram[b * H:(b + 1) * H, :, :, k * G:(k + 1) * G]
                    sp.dma_start(rows.rearrange("h d n t -> (h d) n t"), parts[:, k, :, :]).then_inc(written[k], 16)

            STACK = [(0, 3, 0), (3, 2, 1), (5, 1, 2)]

            def load_q(i, s):
                r = (s % 2) * ROWS
                for at, n, _ in STACK:
                    src = q_dram[ds(i * SLOTS + s, 1), :, 0:n, :].rearrange("a d n t -> (a d) n t")
                    sp.dma_start(q_stack[r + at * DK:r + (at + n) * DK, s, :], src).then_inc(q_loaded[s], 16)

            def load_k(i, s):
                r = (s % 2) * ROWS
                for at, n, part in STACK:
                    src = k_dram[ds(i * SLOTS + s, 1), :, part:part + 1, :].rearrange("a d n t -> (a d) n t")
                    sp.dma_start(k_stack[r + at * DK:r + (at + n) * DK, s // 2, :],
                                 src.broadcast_to([DK, n, S])).then_inc(k_loaded[s // 2], 16)

            for g in range(NG):
                store_parts(g)
                if g == KG:
                    sp.wait_ge(stacks_cleared, 3)
                    for k in range(KG):
                        sp.wait_ge(q_written[k], 2 * 16)
                        sp.wait_ge(k_written[k], 2 * 16)
                if g >= KG:
                    load, s = ((load_k, 0), (load_k, 1), (load_q, 0), (load_q, 1), (load_k, 2), (load_k, 3))[g - KG]
                    load(0, s)
            load_q(0, 2)
            load_q(0, 3)
            for k in range(KG):
                sp.wait_ge(q_written[k], (B + 1) * 16)
                sp.wait_ge(k_written[k], (B + 1) * 16)

            def store_shift(m_count, s):
                sp.wait_ge(nmaxT_evac, 1 + m_count)
                sp.dma_start(q_stack[SHIFT:KROWS, s, :], nmaxT[:, s, :]).then_inc(shift_loaded[s], 16)

            for s in range(AHEAD - 1):
                store_shift(s + 1, s)
            for s in (4, 5):
                load_k(0, s)
                load_q(0, s)

            def attention(i, first=False, last=False, outs=False):
                for s in range(SLOTS):
                    if s == 0:
                        for n, src in enumerate((w1_d[ds(i, 1), :, :].rearrange("e d f -> (e d) f"),
                                                 w2_d[ds(i, 1), :, :].rearrange("e (c f) d -> (e f) c d", f=P))):
                            dst = w12_raw[:, n, :]
                            sp.wait_ge(w_split, i + 1)
                            sp.dma_start(dst if n == 0 else dst.rearrange("p (c d) -> p c d", c=FC), src)\
                              .then_inc(w12_loaded, 16)
                    if not last or s <= SLOTS - AHEAD:
                        store_shift(SLOTS * i + s + AHEAD, (s + AHEAD - 1) % SLOTS)
                    if first and s == 0:
                        for late in (6, 7):
                            load_q(0, late)
                            load_k(0, late)
                    if not last:
                        sp.wait_ge(st_ready, SLOTS * 16 * i + 16 * (s + 1))
                        load_q(i + 1, s)
                        if s % 2:
                            load_k(i + 1, s - 1)
                            load_k(i + 1, s)

            attention(0, first=True)
            attention(1)
            with sp.Fori(2, ITERS - 1) as i:
                attention(i, outs=True)
            attention(ITERS - 1, last=True, outs=True)

            sp.wait_ge(w_rows_ready, 1)
            for half in range(2):
                tiles = w_dram[:, half * NT // 2:(half + 1) * NT // 2, :]
                sp.dma_start(tiles.rearrange("e t p -> t e p"), w_rows[:, half, :]).then_inc(w_written, 16)
            sp.wait_ge(w_written, 32)

            def spread_weights(g, e):
                src = w_dram[e, ds(g * GT, GT), :].rearrange("t p -> (t p)")
                sp.dma_start(w_bc[:, e % WRING, :], src.partition_broadcast(P)).then_inc(w_spread[e % WRING], 16)

            def store_out(g):
                sp.wait_ge(out_ready, 1 + g + 1)
                sp.dma_start(out_v[ds(g, 1), :, :, :].rearrange("g p t d -> (g p) (t d)"),
                             out_sb[:, :, :].rearrange("p t d -> p (t d)")).then_inc(out_stored, 16)

            for e in range(E):
                if e >= WRING:
                    sp.wait_ge(y2_evac, 2 + e - WRING + 1)
                spread_weights(0, e)
            with sp.Fori(1, NG) as g:
                for e in range(E):
                    sp.wait_ge(y2_evac, 2 + g * E + e - WRING + 1)
                    spread_weights(g, e)
                    if e == E - 2:
                        store_out(g - 1)
            store_out(NG - 1)
            sp.wait_ge(out_stored, (NG + 1) * 16)

        @block.gpsimd
        def _(pool):
            pool.sem_inc(h2_low, KG)
            pool.sem_inc(w_split, 1)
            pool.sem_inc(low_pool, FC - 1)
            chain = [0]

            def link(ins):
                chain[0] += 1
                ins.then_inc(pool_chain, 1)
                pool.wait_ge(pool_chain, chain[0])

            link(nc.gpsimd.memset(ident[:, :], 0.0))
            link(nc.gpsimd.memset(ident_b[:, :], 0.0))
            for m in (ident, ident_b):
                nc.gpsimd.affine_select(out=m[:, :], in_=m[:, :], compare_op=ALU.not_equal, fill=1.0,
                                        base=0, pattern=[[-1, P]], channel_multiplier=1).then_inc(ident_made, 1)
            pool.wait_ge(ident_made, 2)
            link(nc.gpsimd.memset(to_rows[:, :, :], 0.0))
            for c in range(2):
                link(nc.gpsimd.affine_select(out=to_rows[:, :, :], in_=to_rows[:, :, :], compare_op=ALU.not_equal,
                                             fill=1.0, base=-2 * 32 * c, pattern=[[-32, 2], [-1, 2 * HW]],
                                             channel_multiplier=1))
            nc.gpsimd.memset(mhalf[:, :], -0.5).then_inc(consts_made, 1)
            pool.wait_ge(consts_made, 1)
            for n, (part, value) in enumerate(((q_stack[:, :, :], 0.0), (k_stack[SHIFT:P, :, :], 1.0),
                                               (v_stage[:, :, :, :], 0.0))):
                nc.gpsimd.memset(part, value).then_inc(stacks_cleared, 1)
                pool.wait_ge(stacks_cleared, n + 1)
            for s in range(SLOTS):
                one = (s % 2) * HW + DK
                last = nc.gpsimd.memset(v_stage[:, s, :, one:one + 1], 1.0)
            link(last)


            def rstd_of(count, *parts):
                pool.wait_ge(var_ready, count)
                every = slice(parts[0].start, parts[-1].stop)
                link(nc.gpsimd.tensor_scalar(vareps[:, every], var[:, 3, every], EPS, None, ALU.add))
                for part in parts:
                    nc.gpsimd.tensor_tensor(rstd[:, part], vareps[:, part], mhalf[:, part],
                                            ALU.pow).then_inc(rstd_ready, 1)

            rstd_of(1, slice(0, KG * GT), slice(KG * GT, NT))
            with pool.Fori(0, B) as b:
                for k in range(KG):
                    g = b * KG + k
                    pool.wait_ge(k_evac, 2 + g + 1)
                    pool.wait_ge(k_written[k], (b + 1) * 16)
                    part = [k_parts[:, k, n, :] for n in range(NPART)]
                    nc.gpsimd.tensor_tensor(kf[:, k, :], kf[:, k, :], part[0], ALU.subtract).then_inc(k_chain, 1)
                    pool.wait_ge(k_second, g + 1)
                    nc.gpsimd.tensor_tensor(part[2], kf[:, k, :], part[1], ALU.subtract).then_inc(k_split, 1)

            def stage_v(i, quad, pv_count):
                wait_apart(pool, pv_done, pv_count)
                W = QUAD * QT * DK
                v_v = v_all[:, ds(i * 2 * W + quad * W, W)].rearrange("p (s a k d) -> p a s k d", a=2, k=QT, d=DK)
                for a in range(2):
                    ins = nc.gpsimd.tensor_copy(v_stage[:, quad * QUAD + a:(quad + 1) * QUAD:2, :, a * HW:a * HW + DK],
                                                v_v[:, a, :, :, :])
                ins.then_inc(v_staged, 1)

            def split_max(m, s):
                wait_apart(pool, mx_free, 2 + QT * (m + 1))
                r1, r2 = nmax_r[:, s, 0, :], nmax_r[:, s, 1, :]
                part = [nmax_p[:, s, n, :] for n in range(NPART)]
                nc.gpsimd.tensor_copy(part[0], nmax[:, s, :]).then_inc(max_chain, 1)
                wait_apart(pool, max_chain, 4 * m + 1)
                nc.gpsimd.tensor_tensor(r1, nmax[:, s, :], part[0], ALU.subtract).then_inc(max_chain, 1)
                wait_apart(pool, max_chain, 4 * m + 2)
                nc.gpsimd.tensor_copy(part[1], r1).then_inc(max_chain, 1)
                wait_apart(pool, max_chain, 4 * m + 3)
                nc.gpsimd.tensor_tensor(r2, r1, part[1], ALU.subtract).then_inc(max_chain, 1)
                wait_apart(pool, max_chain, 4 * m + 4)
                nc.gpsimd.tensor_copy(part[2], r2).then_inc(nmax_split, 1)

            pool.wait_ge(mod_ready, 2)
            pool.wait_ge(w_loaded, W_LOADS * 16)
            pool.wait_ge(wT_ready, 1)
            for b in range(B):
                nc.gpsimd.tensor_tensor(gaboB[:, b, :], gaB[:, b, :], boB[:, :], ALU.mult)
                last = nc.gpsimd.tensor_tensor(wo_ga[:, b, :], gaB[:, b, :], wT[:, 3, :], ALU.mult)
            last.then_inc(wo_ready, 1)
            pool.wait_ge(wo_ready, 1)
            pool.wait_ge(v_evac, 2 + NG)
            stage_v(0, 0, RING)
            for m in range(AHEAD):
                split_max(m, m)

            def attention(i, first=False, last=False, outs=False):
                for s in range(SLOTS):
                    if s == 0:
                        stage_v(i, 1, RING + QT * SLOTS * i)
                    if not last or s < SLOTS - AHEAD:
                        split_max(SLOTS * i + s + AHEAD, (s + AHEAD) % SLOTS)
                    if outs and s == 1:
                        stage_out(i - KG, 0, KG + i - KG)
                    if s == 6:
                        for t in range(GT):
                            xt = x_sb[:, ds(i, 1), t, :].rearrange("p a d -> p (a d)")
                            ins = nc.gpsimd.tensor_tensor(
                                xt, xt, gaboB[:, ds(i // KG, 1), :].rearrange("p a d -> p (a d)"), ALU.add)
                        ins.then_inc(xg_ready, 1)
                    if s == 5:
                        pool.wait_ge(w12_loaded, 32 * (i + 1))
                        for n, w in enumerate((w1, w2)):
                            high, low = (w[:, j, ds(i, 1), :].rearrange("p a f -> p (a f)") for j in range(2))
                            nc.gpsimd.tensor_copy(high, w12_raw[:, n, :]).then_inc(ws_chain, 1)
                            pool.wait_ge(ws_chain, 2 * i + n + 1)
                            ins = nc.gpsimd.tensor_tensor(low, w12_raw[:, n, :], high.bitcast(F32), ALU.subtract)
                        ins.then_inc(w_split, 1)
                    if s == QUAD and not last:
                        stage_v(i + 1, 0, RING + QT * (SLOTS * i + QUAD))

            def stage_out(g, slot, transposed):
                b = g // KG
                HALF_OUTS = H // 2
                wait_apart(pool, o_done, 1 + (b + 1) * HALF_OUTS)
                wait_apart(pool, ao_ready, transposed)
                W = KG * GT * 2 * DK
                o_v = o_all[:, :, :, :, :].rearrange("p o k t e -> p (o k t e)")
                src = o_v[:, ds(b * (HALF_OUTS * W - W) + g * (W // KG), HALF_OUTS * W)].rearrange(
                    "p (o k x) -> p k o x", o=HALF_OUTS, k=KG)[:, 0, :, :]
                nc.gpsimd.tensor_copy(o_st[:, slot, :].rearrange("p (t o e) -> p o t e", t=GT, o=HALF_OUTS),
                                      src.rearrange("p o (t e) -> p o t e", t=GT)).then_inc(o_staged, 1)

            attention(0, first=True)
            attention(1)
            with pool.Fori(2, ITERS - 1) as i:
                attention(i, outs=True)
            attention(ITERS - 1, last=True, outs=True)

            rstd_of(2, slice(0, LATE))
            for k in range(KG):
                stage_out(NG - KG + k, k, NG)
            rstd_of(3, slice(LATE, NT))
            with pool.Fori(0, B) as b:
                for k in range(KG):
                    g = b * KG + k
                    pool.wait_ge(h2_ready, 2 + g + 1)
                    one = [h2[:, j, ds(g * G, G)] for j in range(2)]
                    nc.gpsimd.tensor_tensor(one[1], hT[:, k, :], one[0].bitcast(F32), ALU.subtract).then_inc(h2_low, 1)
            with pool.Fori(0, NG) as g:
                for e in range(E):
                    for fc in range(FC - 1):
                        pool.wait_ge(gelu_done, 4 + (g * E + e) * FC + fc + 1)
                        u = (e % 2) * FC + fc
                        nc.gpsimd.tensor_tensor(hid_hl[:, 1, u, :], hid[:, fc, :], hid_hl[:, 0, u, :].bitcast(F32),
                                                ALU.subtract).then_inc(low_pool, 1)

        @block.scalar
        def _(act):
            act.sem_inc(hT_ready, 2)
            act.sem_inc(q_evac, 2)
            act.sem_inc(k_evac, 2)
            act.sem_inc(exp_done, 2)
            act.sem_inc(pv_evac, 1)
            act.sem_inc(nmaxT_evac, 1)
            act.sem_inc(h2_ready, 2)
            act.sem_inc(ao_evac, 2)
            act.sem_inc(gelu_done, 4)
            act.sem_inc(gated, 1)
            act.wait_ge(small_loaded, 32)
            nc.scalar.activation(silu_t[:, 0, :], cT[:, :], ACT.Exp, scale=-1.0).then_inc(c_exp_done, 1)
            act.wait_ge(w_transposed, 1)
            nc.scalar.activation(wT[:, :, :].rearrange("p a b -> p (a b)"), bank(0), ACT.Copy).then_inc(wT_ready, 1)
            nc.scalar.activation(b1c[:, :], bank(1)[:, 0:E * FC], ACT.Copy).then_inc(wT_ready, 1)
            nc.scalar.activation(b2c[:, :], bank(1)[:, E * FC:E * FC + E], ACT.Copy).then_inc(wT_ready, 1)
            act.wait_ge(mod_ready, 1)
            act.wait_ge(w_loaded, W_LOADS * 16)

            def modulate(g, k, b):
                wait_apart(act, xT_ready, 2 + g + 1)
                nc.scalar.activation(hT[:, k, :], bank(k), ACT.Identity,
                                     bias=mod_c[:, 0, ds(b, 1)], scale=mod_c[:, 1, ds(b, 1)]).then_inc(hT_ready, 1)

            def project(g, k, b):
                for mm_done, split, written, full, parts, src, bias, evac in (
                        (q_mm, q_split, q_written, qf, q_parts, 2, bq, q_evac),
                        (k_mm, k_split, k_written, kf, k_parts, 4, bk, k_evac)):
                    act.wait_ge(mm_done, g + 1)
                    act.wait_ge(split, g + 1)
                    nc.scalar.activation(full[:, k, :], bank(src + k), ACT.Identity, bias=bias[:, :])
                    act.wait_ge(written[k], (b + 1) * 16)
                    nc.scalar.activation(parts[:, k, 0, :], bank(src + k), ACT.Identity,
                                         bias=bias[:, :]).then_inc(evac, 1)

            def second_part(g, k):
                wait_apart(act, k_chain, g + 1)
                nc.scalar.activation(k_parts[:, k, 1, :], kf[:, k, :], ACT.Copy).then_inc(k_second, 1)

            modulate(0, 0, 0)
            modulate(1, 1, 0)
            project(0, 0, 0)
            with act.Fori(0, B - 1) as b:
                for k in range(KG):
                    g = b * KG + k
                    modulate(g + 2, k, b + 1)
                    second_part(g, k)
                    project(g + 1, 1 - k, b + k)
            project(NG - 1, 1, B - 1)
            second_part(NG - 2, 0)
            second_part(NG - 1, 1)

            def evac_shift(m, s):
                act.wait_ge(nmaxT_ready, m + 1)
                nc.scalar.activation(nmaxT[:, s, :], bank(MISC)[0:NPART * QT, 0:P // 2].bitcast(BF16),
                                     ACT.Copy).then_inc(nmaxT_evac, 1)

            def evac_pv(n, s):
                act.wait_ge(pv_done, RING + QT * n)
                nc.scalar.activation(pv_sb[:, s // 2 % 2, :], bank(PV), ACT.Copy).then_inc(pv_evac, 1)

            def evac_out(g, slot, from_bank):
                act.wait_ge(ao_ready, KG + g + 1)
                nc.scalar.activation(oT[:, slot, :], bank(from_bank), ACT.Copy).then_inc(ao_evac, 1)

            for m in range(AHEAD - 1):
                evac_shift(m, m)

            def attention(i, first=False, last=False, outs=False):
                for s in range(SLOTS):
                    n = SLOTS * i + s
                    for kt in range(QT):
                        act.wait_ge(pv_done, QT * n + kt + 1)
                        for half in range(2):
                            if kt == 1 and half == 1 and s % 2 == 0 and not (first and s == 0):
                                evac_pv(n, (s - 2) % SLOTS)
                            if outs and s == 3 and kt == 6 and half == 1:
                                evac_out(i - KG, 0, MISC)
                            if kt == 3 and half == 1 and (not last or s <= SLOTS - AHEAD):
                                evac_shift(n + AHEAD - 1, (s + AHEAD - 1) % SLOTS)
                            act.wait_ge(st_ready, 16 * n + 2 * kt + half + 1)
                            nc.scalar.activation(probs[:, kt % RING, half * 512:(half + 1) * 512],
                                                 st_bank(kt, half, last and s >= SLOTS - AHEAD),
                                                 ACT.Exp, scale=SCALE).then_inc(exp_done, 1)
                if last:
                    evac_pv(SLOTS * i + SLOTS, SLOTS - 2)

            attention(0, first=True)
            attention(1)
            with act.Fori(2, ITERS - 1) as i:
                attention(i, outs=True)
            attention(ITERS - 1, last=True, outs=True)

            for k in range(KG):
                evac_out(NG - KG + k, k, k)
            act.wait_ge(o_staged, NG)
            with act.Fori(0, B) as b:
                for k in range(KG):
                    g = b * KG + k
                    act.wait_ge(x2T_ready, 2 + g + 1)
                    wait_apart(act, h2_low, (b + 1) * KG)
                    nc.scalar.activation(hT[:, k, :], bank(4 + k), ACT.Identity,
                                         bias=mod_c[:, 3, ds(b, 1)], scale=mod_c[:, 4, ds(b, 1)])
                    nc.scalar.activation(h2[:, 0, ds(g * G, G)], bank(4 + k), ACT.Identity,
                                         bias=mod_c[:, 3, ds(b, 1)], scale=mod_c[:, 4, ds(b, 1)]).then_inc(h2_ready, 1)
            def hidden(g, e):
                unit = g * E + e
                for fc in range(FC):
                    n, u = e * FC + fc, (e % 2) * FC + fc
                    act.wait_ge(h_mm, g * E * FC + n + 1)
                    if fc == 0:
                        act.wait_ge(y2_mm, unit + 1)
                    if fc < FC - 1:
                        act.wait_ge(low_pool, unit * (FC - 1) + fc + 1)
                    else:
                        act.wait_ge(low_dve, unit + 1)
                    nc.scalar.activation(hid[:, fc, :], bank(n % 4), ACT.Gelu, bias=b1c[:, n:n + 1])
                    nc.scalar.activation(hid_hl[:, 0, u, :], bank(n % 4), ACT.Gelu,
                                         bias=b1c[:, n:n + 1]).then_inc(gelu_done, 1)

            def experts(g):
                for e in range(E):
                    hidden(g, e)
                    if e == 1:
                        gate(g - 1)

            def gate(g):
                wait_apart(act, y2_evac, 2 + (g + 1) * E)
                nc.scalar.activation(acc_gb[:, :], acc[:, :], ACT.Copy,
                                     scale=gb_c[:, 0, ds(g // KG, 1)]).then_inc(gated, 1)

            hidden(0, 0)
            act.wait_ge(logit_gap, 1)
            nc.scalar.activation(wts[:, 1, :], wts[:, 0, :], ACT.Exp).then_inc(gap_exp, 1)
            hidden(0, 1)
            for e in range(2, E):
                hidden(0, e)
            with act.Fori(1, NG) as g:
                experts(g)
            gate(NG - 1)

        @block.vector
        def _(dve):
            dve.sem_inc(o_done, 1)
            dve.sem_inc(q_split, 2)
            dve.sem_inc(k_split, 2)
            dve.sem_inc(v_evac, 2)
            dve.sem_inc(mx_free, 2)
            dve.sem_inc(y2_evac, 2)
            dve.sem_inc(low_dve, 1)
            dve.sem_inc(out_ready, 1)
            dve.sem_inc(g_evac, 2)
            dve.sem_inc(x2_ready, 2)
            chain = [0]

            def link(ins):
                chain[0] += 1
                ins.then_inc(dve_chain, 1)
                dve.wait_ge(dve_chain, chain[0])

            for e in range(E):
                last = nc.vector.memset(iota_e[:, e:e + 1], float(e))
            def silu():
                dve.wait_ge(c_exp_done, 1)
                link(nc.vector.tensor_scalar(silu_t[:, 1, :], silu_t[:, 0, :], 1.0, None, ALU.add))
                link(nc.vector.reciprocal(silu_t[:, 0, :], silu_t[:, 1, :]))
                link(nc.vector.tensor_tensor(siluT[:, :], cT[:, :], silu_t[:, 0, :], ALU.mult))
                for b in range(B):
                    last = nc.vector.tensor_copy(silu_b[:, b, :], siluT[:, b:b + 1].broadcast_to([P, P]))
                last.then_inc(silu_done, 1)

            def modulation():
                dve.wait_ge(mod_done, 1)
                modp = bank(2)[:, 0:MOD * B].rearrange("p (m b) -> p m b", b=B)
                link(nc.vector.tensor_copy(mod_c[:, :, :], modp))
                for m in (1, 4):
                    last = nc.vector.tensor_scalar(mod_c[:, m, :], mod_c[:, m, :], 1.0, None, ALU.add)
                last.then_inc(mod_ready, 1)

            def gates():
                dve.wait_ge(w_loaded, W_LOADS * 16)
                dve.wait_ge(mod_ready, 1)
                link(nc.vector.reciprocal(rtemp[:, :], tempB[:, :]))
                for src, t0, t1, dst in (
                        (bank(3), gate_t[:, 0, :, :].rearrange("p b d -> p (b d)"),
                         gate_t[:, 1, :, :].rearrange("p b d -> p (b d)"), gaB[:, :, :].rearrange("p b d -> p (b d)")),
                        (mod_c[:, 5, :], gb_c[:, 1, :], gb_c[:, 2, :], gb_c[:, 0, :])):
                    link(nc.vector.tensor_scalar(t0, src, 0.0, 2.0, ALU.is_ge, ALU.mult))
                    link(nc.vector.tensor_scalar(t1, src, -1.0, None, ALU.mult))
                    link(nc.vector.tensor_tensor(t1, src, t1, ALU.max))
                    link(nc.vector.tensor_scalar(t1, t1, 0.25, None, ALU.max))
                    last = nc.vector.scalar_tensor_tensor(dst, t0, -1.0, t1, ALU.add, ALU.mult)
                last.then_inc(mod_ready, 1)

            def rows(g, t):
                return x_sb[:, ds(g, 1), t, :].rearrange("p a d -> p (a d)")

            def row_stats(g, tiles=range(GT)):
                for t in tiles:
                    ins = nc.vector.bn_stats(stats[:, ds(g * GT + t, 1), :].rearrange("p a n -> p (a n)"), rows(g, t))
                return ins

            def row_moments(part=slice(0, NT)):
                m0, v0, m1, v1 = (stats[:, part, n] for n in (1, 2, 4, 5))
                link(nc.vector.tensor_tensor(mean[:, part], m0, m1, ALU.add))
                link(nc.vector.tensor_tensor(var[:, 0, part], m0, m1, ALU.subtract))
                link(nc.vector.tensor_tensor(var[:, 1, part], v0, v1, ALU.add))
                link(nc.vector.tensor_tensor(var[:, 2, part], var[:, 0, part], var[:, 0, part], ALU.mult))
                link(nc.vector.tensor_scalar(var[:, 0, part], var[:, 2, part], 0.25, None, ALU.mult))
                nc.vector.scalar_tensor_tensor(var[:, 3, part], var[:, 1, part], 1.0 / D, var[:, 0, part],
                                               ALU.mult, ALU.add).then_inc(var_ready, 1)
                link(nc.vector.tensor_scalar(mean[:, part], mean[:, part], 0.5, None, ALU.mult))

            def normalise_rows(g, k, done, transposed):
                dve.wait_ge(transposed, g + 1)
                for t in range(GT):
                    one = [a[:, ds(g * GT + t, 1)] for a in (mean, rstd)]
                    ins = nc.vector.tensor_scalar(xn[:, k, t, :], rows(g, t), one[0], one[1], ALU.subtract, ALU.mult)
                ins.then_inc(done, 1)

            silu()
            for half in range(2):
                dve.wait_ge(x_loaded[half], 16)
                with dve.Fori(half * B // 2, (half + 1) * B // 2) as b:
                    for k in range(KG):
                        ins = row_stats(b * KG + k)
                    ins.then_inc(stats_done, KG)
            dve.wait_ge(stats_done, NG)
            row_moments()
            modulation()
            dve.wait_ge(rstd_ready, 1)
            HQ = H * QT * DK

            def split_qv(g, k, b):
                dve.wait_ge(v_mm, g + 1)
                v_v = v_all[:, ds(b * HQ, HQ)].rearrange("p (h k d) -> p k h d", h=H, k=QT)
                for t in range(GT):
                    ins = nc.vector.tensor_tensor(
                        v_v[:, k * GT + t, :, :],
                        bank(6 + k)[:, t * D:(t + 1) * D].rearrange("p (h d) -> p h d", h=H),
                        bvB[:, :].rearrange("p (h d) -> p h d", h=H), ALU.add)
                ins.then_inc(v_evac, 1)
                dve.wait_ge(q_evac, 2 + g + 1)
                dve.wait_ge(q_written[k], (b + 1) * 16)
                part = [q_parts[:, k, n, :] for n in range(NPART)]
                nc.vector.tensor_tensor(qf[:, k, :], qf[:, k, :], part[0], ALU.subtract).then_inc(q_chain, 1)
                dve.wait_ge(q_chain, g * 2 + 1)
                nc.vector.tensor_copy(part[1], qf[:, k, :]).then_inc(q_chain, 1)
                dve.wait_ge(q_chain, g * 2 + 2)
                nc.vector.tensor_tensor(part[2], qf[:, k, :], part[1], ALU.subtract).then_inc(q_split, 1)

            def qkv_rows(g, k):
                normalise_rows(g, k, xn_ready, xT_ready)

            qkv_rows(0, 0)
            qkv_rows(1, 1)
            gates()
            dve.wait_ge(rstd_ready, 2)
            with dve.Fori(0, B - 1) as b:
                for k in range(KG):
                    qkv_rows(b * KG + k + 2, k)
                    split_qv(b * KG + k, k, b)
            split_qv(NG - 2, 0, B - 1)
            split_qv(NG - 1, 1, B - 1)

            def reduce_max(m, s, qt):
                dve.wait_ge(mx_ready, QT * m + qt + 1)
                nc.vector.tensor_reduce(nmax[:, s, qt:qt + 1], bank(2 + 2 * (qt % 2), 2), AX.X, ALU.max,
                                        negate=True).then_inc(mx_free, 1)

            def row_sums(m, s):
                dve.wait_ge(oT_ready, m + 1)
                o_ps = bank(MISC)[:, 0:GT * 4 * HW].rearrange("p (x e) -> p x e", e=HW)
                nc.vector.reciprocal(rsum[:, s // 2 % 2, :], o_ps[:, :, DK]).then_inc(rsum_ready, 1)

            def normalise(m, s):
                dve.wait_ge(rsum_ready, m + 1)
                o_ps = bank(MISC)[:, 0:GT * 4 * HW].rearrange("p (x e) -> p x e", e=HW)
                nc.vector.tensor_tensor(
                    o_all[:, ds(m, 1), :, :, :].rearrange("p o k t (a d) -> p (o k t a) d", a=2),
                    o_ps[:, :, 0:DK],
                    rsum[:, s // 2 % 2, :].rearrange("p (x a) -> p x a", a=1).broadcast_to([P, 4 * GT, DK]),
                    ALU.mult).then_inc(o_done, 1)

            def residual(g, from_bank):
                dve.wait_ge(y_mm, g + 1)
                dve.wait_ge(xg_ready, g + 1)
                xg = x_sb[:, ds(g, 1), :, :].rearrange("p a t d -> p (a t d)")
                nc.vector.tensor_tensor(xg, bank(from_bank), xg, ALU.add).then_inc(x2_ready, 1)

            for m in range(AHEAD):
                for qt in range(QT):
                    reduce_max(m, m, qt)

            def attention(i, first=False, last=False, outs=False):
                for s in range(SLOTS):
                    for kt in range(QT):
                        if not last or s < SLOTS - AHEAD:
                            reduce_max(SLOTS * i + s + AHEAD, (s + AHEAD) % SLOTS, kt)
                        if outs and s == 5 and kt == 7:
                            residual(i - KG, MISC)
                        if outs and s == 7 and kt >= GT:
                            if kt == GT:
                                wait_apart(dve, x2_ready, 2 + i - KG + 1)
                            ins = row_stats(i - KG, [kt - GT])
                            if kt == QT - 1:
                                ins.then_inc(stats_done, 1)
                                if last:
                                    dve.wait_ge(stats_done, 2 * NG - KG)
                                    row_moments(slice(0, LATE))
                        if s % 2 == 0 and not (first and s == 0):
                            m = SLOTS // 2 * i + s // 2 - 1
                            if kt == 4:
                                row_sums(m, (s - 2) % SLOTS)
                            if kt == 5:
                                normalise(m, (s - 2) % SLOTS)
                if last:
                    row_sums(OUTS - 1, SLOTS - 2)
                    normalise(OUTS - 1, SLOTS - 2)

            attention(0, first=True)
            attention(1)
            with dve.Fori(2, ITERS - 1) as i:
                attention(i, outs=True)
            attention(ITERS - 1, last=True, outs=True)

            def h2_rows(g, k):
                normalise_rows(g, k, xn2_ready, x2T_ready)

            dve.wait_ge(rstd_ready, 3)
            h2_rows(0, 0)
            h2_rows(1, 1)
            for k in range(KG):
                g = NG - KG + k
                residual(g, 2 + k)
                dve.wait_ge(x2_ready, 2 + g + 1)
                row_stats(g).then_inc(stats_done, 1)
            dve.wait_ge(stats_done, 2 * NG)
            row_moments(slice(LATE, NT))

            def router(g, k):
                dve.wait_ge(g_mm, g + 1)
                nc.vector.tensor_tensor(logits[:, ds(g * GT, GT), :],
                                        bank(6 + k)[:, 0:GT * E].rearrange("p (t e) -> p t e", e=E),
                                        gbiasB[:, :].rearrange("p (a e) -> p a e", a=1).broadcast_to([P, GT, E]),
                                        ALU.add).then_inc(g_evac, 1)

            with dve.Fori(0, B - 2) as b:
                for k in range(KG):
                    h2_rows(b * KG + k + 2, k)
                    router(b * KG + k, k)
            dve.wait_ge(rstd_ready, 4)
            for k in range(KG):
                h2_rows(NG - KG + k, k)
                router(NG - 2 * KG + k, k)
            router(NG - 2, 0)
            router(NG - 1, 1)
            dve.wait_ge(g_evac, 2 + NG)
            lg = logits[:, :, :].rearrange("p t e -> p (t e)")
            link(nc.vector.tensor_scalar(lg, lg, rtemp[:, :], None, ALU.mult))
            for t in range(NT):
                last = nc.vector.max(eight_v[:, t, :], logits[:, t, :])
            link(last)
            for t in range(NT):
                last = nc.vector.max_index(eight_i[:, t, :], eight_v[:, t, :], logits[:, t, :])
            link(last)
            for n in range(2):
                last = nc.vector.tensor_copy(top_if[:, n, :], eight_i[:, :, n])
            link(last)
            def low_part(g, e):
                dve.wait_ge(gelu_done, 4 + (g * E + e + 1) * FC)
                u = (e % 2) * FC + FC - 1
                nc.vector.tensor_tensor(hid_hl[:, 1, u, :], hid[:, FC - 1, :], hid_hl[:, 0, u, :].bitcast(F32),
                                        ALU.subtract).then_inc(low_dve, 1)

            nc.vector.tensor_tensor(wts[:, 0, :], eight_v[:, :, 1], eight_v[:, :, 0], ALU.subtract).then_inc(logit_gap, 1)
            low_part(0, 0)
            dve.wait_ge(gap_exp, 1)
            link(nc.vector.tensor_scalar(wts[:, 2, :], wts[:, 1, :], 1.0, None, ALU.add))
            link(nc.vector.reciprocal(wts[:, 3, :], wts[:, 2, :]))
            link(nc.vector.tensor_tensor(wts[:, 2, :], wts[:, 1, :], wts[:, 3, :], ALU.mult))
            def each(a):
                return a.rearrange("p (t a) -> p t a", a=1).broadcast_to([P, NT, E])

            experts_of = iota_e[:, :].rearrange("p (a e) -> p a e", a=1).broadcast_to([P, NT, E])
            for n in range(2):
                last = nc.vector.tensor_tensor(hot[:, n, :, :], experts_of, each(top_if[:, n, :]), ALU.is_equal)
            link(last)
            for n, w in ((0, 3), (1, 2)):
                last = nc.vector.tensor_tensor(hot[:, n, :, :], hot[:, n, :, :], each(wts[:, w, :]), ALU.mult)
            link(last)
            flat = [a.rearrange("p t e -> p (t e)") for a in (w_exp[:, :, :], hot[:, 0, :, :], hot[:, 1, :, :])]
            nc.vector.tensor_tensor(flat[0], flat[1], flat[2], ALU.add).then_inc(w_ready, 1)
            dve.wait_ge(w_rows_mm, 1)
            nc.vector.tensor_copy(w_rows[:, :, :].rearrange("p a b -> p (a b)"), bank(6)[:, 0:2 * P])\
              .then_inc(w_rows_ready, 1)

            def combine(g, e):
                unit = g * E + e
                dve.wait_ge(y2_mm, 2 + unit + 1)
                dve.wait_ge(w_spread[e % WRING], (g * (E // WRING) + e // WRING + 1) * 16)
                if e == 0:
                    dve.wait_ge(gated, g + 1)
                    nc.vector.scalar_tensor_tensor(acc[:, :], bank(4 + e % 2), b2c[:, e:e + 1], w_bc[:, e % WRING, :],
                                                   ALU.add, ALU.mult).then_inc(y2_evac, 1)
                else:
                    nc.vector.scalar_tensor_tensor(acc_t[:, :], bank(4 + e % 2), b2c[:, e:e + 1], w_bc[:, e % WRING, :],
                                                   ALU.add, ALU.mult).then_inc(acc_chain, 1)
                    dve.wait_ge(acc_chain, g * (E - 1) + e)
                    dve.wait_ge(y2_evac, 2 + unit)
                    nc.vector.tensor_tensor(acc[:, :], acc[:, :], acc_t[:, :], ALU.add).then_inc(y2_evac, 1)

            def finish(g):
                dve.wait_ge(outT_mm, g + 1)
                dve.wait_ge(out_stored, (g + 1) * 16)
                nc.vector.tensor_tensor(out_sb[:, :, :].rearrange("p t d -> p (t d)"), bank(7),
                                        x_sb[:, ds(g, 1), :, :].rearrange("p a t d -> p (a t d)"),
                                        ALU.add).then_inc(out_ready, 1)

            def experts(g, start=0):
                for e in range(start, E):
                    if e == 2 and start:
                        combine(0, 0)
                    combine(g if e else g - 1, (e - 1) % E)
                    low_part(g, e)
                    if e == 3 and not start:
                        finish(g - 1)

            low_part(0, 1)
            experts(0, start=2)
            with dve.Fori(1, NG) as g:
                experts(g)
            combine(NG - 1, E - 1)
            finish(NG - 1)

        @block.tensor
        def _(pe):
            mm = nc.tensor.matmul
            pe.sem_inc(pv_done, RING)
            pe.sem_inc(y2_mm, 2)
            pe.sem_inc(ao_ready, KG)
            pe.sem_inc(xT_ready, 2)
            pe.sem_inc(x2T_ready, 2)
            pe.wait_ge(silu_done, 1)
            for m in range(MOD):
                mm(bank(2)[:, m * B:(m + 1) * B], wmod[:, m * D:(m + 1) * D], siluT[:, :], start=True, stop=True)
            for b in range(B):
                last = mm(bank(3)[:, b * D:(b + 1) * D], silu_b[:, b, :], wmod[:, 2 * D:3 * D], start=True, stop=True)
            last.then_inc(mod_done, 1)
            pe.wait_ge(ident_made, 2)
            pe.wait_ge(w_loaded, W_LOADS * 16)
            for n in range(4):
                nc.tensor.transpose(bank(0)[:, n * D:(n + 1) * D], w_raw[:, n, :], ident[:, :])
            nc.tensor.transpose(bank(1)[:, 0:E * FC], b1_raw[:, :], ident[0:E * FC, 0:E * FC])
            nc.tensor.transpose(bank(1)[:, E * FC:E * FC + E], b2_raw[:, :], ident[0:E, 0:E]).then_inc(w_transposed, 1)
            pe.wait_ge(wT_ready, 3)
            pe.wait_ge(mod_ready, 1)

            def transpose_rows(g, k, base, ready, read, done):
                pe.wait_ge(ready, g + 1)
                pe.wait_ge(read, g + 1)
                for t in range(GT):
                    ins = nc.tensor.transpose(bank(base + k)[:, t * P:(t + 1) * P], xn[:, k, t, :], ident[:, :])
                ins.then_inc(done, 1)

            def qkv(g, k):
                pe.wait_ge(hT_ready, 2 + g + 1)
                pe.wait_ge(q_evac, g + 1)
                mm(bank(2 + k), wT[:, 0, :], hT[:, k, :], start=True, stop=True).then_inc(q_mm, 1)
                pe.wait_ge(k_evac, g + 1)
                mm(bank(4 + k), wT[:, 1, :], hT[:, k, :], start=True, stop=True).then_inc(k_mm, 1)
                pe.wait_ge(v_evac, g + 1)
                for t in range(GT):
                    ins = mm(bank(6 + k)[:, t * D:(t + 1) * D], hT[:, k, t * P:(t + 1) * P], wT[:, 2, :],
                             start=True, stop=True)
                ins.then_inc(v_mm, 1)

            def x_rows(g, k):
                transpose_rows(g, k, 0, xn_ready, hT_ready, xT_ready)

            x_rows(0, 0)
            with pe.Fori(0, B - 1) as b:
                x_rows(b * KG + 1, 1)
                qkv(b * KG, 0)
                x_rows(b * KG + 2, 0)
                pe.wait_ge(mod_ready, 2)
                qkv(b * KG + 1, 1)
            x_rows(NG - 1, 1)
            qkv(NG - 2, 0)
            qkv(NG - 1, 1)
            pe.wait_ge(q_evac, 2 + NG)
            pe.wait_ge(k_evac, 2 + NG)
            pe.wait_ge(v_evac, 2 + NG)

            def scores_for_max(i, s, m, qt):
                if qt == 0:
                    pe.wait_ge(q_loaded[s], 3 * 16 * (i + 1))
                    pe.wait_ge(k_loaded[s // 2], 2 * 3 * 16 * (i + 1))
                pe.wait_ge(mx_free, QT * m + qt + 1)
                for half in range(2):
                    last = mm(bank(2 + 2 * (qt % 2) + half), q_stack[0:SHIFT, s, qt * P:(qt + 1) * P],
                              k_stack[0:SHIFT, s // 2, half * 512:(half + 1) * 512], start=True, stop=True)
                last.then_inc(mx_ready, 1)

            def scores(i, s, kt, half, alone):
                n = SLOTS * i + s
                if kt == 0 and half == 0:
                    pe.wait_ge(shift_loaded[s], 16 * (i + 1))
                free = 2 + 16 * n + 2 * kt + half + 1 - 2
                if alone and kt == 1 and s == SLOTS - AHEAD:
                    pe.wait_ge(mx_free, 2 + QT * B * H)
                if alone and (kt or s > SLOTS - AHEAD):
                    free -= 2
                pe.wait_ge(exp_done, free)
                mm(st_bank(kt, half, alone), k_stack[0:KROWS, s // 2, kt * P:(kt + 1) * P],
                   q_stack[0:KROWS, s, half * 512:(half + 1) * 512], start=True, stop=True).then_inc(st_ready, 1)

            def transpose_shift(m, s, o_count):
                pe.wait_ge(nmax_split, m + 1)
                pe.wait_ge(o_done, 1 + o_count)
                pe.wait_ge(nmaxT_evac, 1 + m)
                nc.tensor.transpose(bank(MISC)[0:NPART * QT, 0:P // 2].bitcast(BF16),
                                    nmax_p[:, s, :, :].rearrange("p n t -> p (n t)"), ident_b[:, :])\
                  .then_inc(nmaxT_ready, 1)

            def transpose_out(m, s, shift_count):
                pe.wait_ge(pv_evac, 1 + m + 1)
                pe.wait_ge(nmaxT_evac, 1 + shift_count)
                pe.wait_ge(o_done, 1 + m)
                for t in range(GT):
                    o_ps = bank(MISC)[:, 0:GT * 4 * HW].rearrange("p (h t e) -> p h t e", h=2, t=GT)
                    last = mm(o_ps[:, :, t, :], pv_sb[:, s // 2 % 2, t * P:(t + 1) * P],
                              to_rows[:, :, :].rearrange("p h e -> p (h e)"), start=True, stop=True)
                last.then_inc(oT_ready, 1)

            def pv(i, s, kt):
                n = SLOTS * i + s
                pe.wait_ge(exp_done, 2 + 16 * n + 2 * kt + 4)
                if kt == 0:
                    if s % 2 == 0:
                        pe.wait_ge(pv_evac, 1 + SLOTS // 2 * i + s // 2)
                    if s % QUAD == 0:
                        pe.wait_ge(v_staged, 2 * i + s // QUAD + 1)
                for c in range(2):
                    for h in range(2):
                        j = 2 * c + h
                        last = mm(bank(PV)[32 * j:32 * j + 32, :], v_stage[:, s, kt + c, :],
                                  probs[:, (kt + c) % RING, h * 512:(h + 1) * 512],
                                  start=kt == 0 and s % 2 == 0, stop=kt == QT - 2 and s % 2 == 1)
                last.then_inc(pv_done, 2)

            pe.wait_ge(stacks_cleared, 3)
            for m in range(AHEAD):
                for qt in range(QT):
                    if m and qt == QT // 2:
                        transpose_shift(m - 1, m - 1, 0)
                    scores_for_max(0, m, m, qt)

            def features_first(g, slot, to_bank):
                pe.wait_ge(o_staged, g + 1)
                for t in range(GT):
                    ins = nc.tensor.transpose(bank(to_bank)[:, t * P:(t + 1) * P], o_st[:, slot, t * D:(t + 1) * D],
                                              ident[:, :])
                ins.then_inc(ao_ready, 1)

            def project_out(g, slot, to_bank):
                pe.wait_ge(wo_ready, 1)
                pe.wait_ge(ao_evac, 2 + g + 1)
                for t in range(GT):
                    ins = mm(bank(to_bank)[:, t * D:(t + 1) * D], oT[:, slot, t * P:(t + 1) * P],
                             wo_ga[:, ds(g // KG, 1), :].rearrange("p a d -> p (a d)"), start=True, stop=True)
                ins.then_inc(y_mm, 1)

            def attention(i, first=False, last=False, outs=False):
                for s in range(SLOTS):
                    n = SLOTS * i + s

                    def ahead(qt):
                        if not last or s < SLOTS - AHEAD:
                            scores_for_max(i + (s + AHEAD) // SLOTS, (s + AHEAD) % SLOTS, n + AHEAD, qt)

                    alone = last and s >= SLOTS - AHEAD
                    for kt in range(0, QT, 2):
                        scores(i, s, kt, 0, alone)
                        ahead(kt)
                        ahead(kt + 1)
                        scores(i, s, kt, 1, alone)
                        scores(i, s, kt + 1, 0, alone)
                        if outs and kt == 2 and s == 4:
                            pe.wait_ge(ao_evac, 2 + i - KG + 1)
                        if outs and kt == 2 and s == 6:
                            pe.wait_ge(x2_ready, 2 + i - KG + 1)
                        if kt == 2 and (not last or s <= SLOTS - AHEAD):
                            read = SLOTS // 2 * i + (s - 1) // 2
                            transpose_shift(n + AHEAD - 1, (s + AHEAD - 1) % SLOTS, 0 if first and s == 0 else read)
                        if kt == 4 and s % 2 == 0 and not (first and s == 0):
                            transpose_out(SLOTS // 2 * i + s // 2 - 1, (s - 2) % SLOTS,
                                          min(n + AHEAD, B * H) if last else n + AHEAD)
                        if kt:
                            pv(i, s, kt - 2)
                        elif not (first and s == 0):
                            pv(i if s else i - 1, (s - 1) % SLOTS, QT - 2)
                        scores(i, s, kt + 1, 1, alone)
                        if outs and kt == 4 and s in (3, 5):
                            pe.wait_ge(nmaxT_evac, 1 + n + AHEAD)
                            pe.wait_ge(o_done, 1 + SLOTS // 2 * i + s // 2)
                            if s == 3:
                                features_first(i - KG, 0, MISC)
                            else:
                                project_out(i - KG, 0, MISC)
                if last:
                    pv(i, SLOTS - 1, QT - 2)
                    transpose_out(OUTS - 1, SLOTS - 2, B * H)

            attention(0, first=True)
            attention(1)
            with pe.Fori(2, ITERS - 1) as i:
                attention(i, outs=True)
            attention(ITERS - 1, last=True, outs=True)
            pe.wait_ge(o_done, 1 + OUTS)

            def h2_rows(g, k):
                transpose_rows(g, k, 4, xn2_ready, h2_ready, x2T_ready)

            def router(g, k):
                pe.wait_ge(h2_ready, 2 + g + 1)
                pe.wait_ge(g_evac, g + 1)
                for t in range(GT):
                    ins = mm(bank(6 + k)[:, t * E:(t + 1) * E], hT[:, k, t * P:(t + 1) * P], gate_w[:, :],
                             start=True, stop=True)
                ins.then_inc(g_mm, 1)

            h2_rows(0, 0)
            for k in range(KG):
                features_first(NG - KG + k, k, k)
            for k in range(KG):
                project_out(NG - KG + k, k, 2 + k)
            with pe.Fori(0, B - 1) as b:
                h2_rows(b * KG + 1, 1)
                router(b * KG, 0)
                h2_rows(b * KG + 2, 0)
                router(b * KG + 1, 1)
            h2_rows(NG - 1, 1)
            router(NG - 2, 0)
            router(NG - 1, 1)
            pe.wait_ge(g_evac, 2 + NG)
            pe.wait_ge(h2_low, KG + NG)
            pe.wait_ge(w_split, 1 + E)
            PASSES = ((0, 0), (1, 0), (0, 1))

            def up(g, e):
                for fc in range(FC):
                    n = e * FC + fc
                    pe.wait_ge(gelu_done, g * E * FC + n + 1)
                    for j, (a, b) in enumerate(PASSES):
                        ins = mm(bank(n % 4), w1[:, a, e, fc * P:(fc + 1) * P], h2[:, b, ds(g * G, G)],
                                 start=j == 0, stop=j == 2)
                    ins.then_inc(h_mm, 1)

            def down(g, e):
                unit = g * E + e
                pe.wait_ge(y2_evac, unit + 1)
                for fc in range(FC):
                    pe.wait_ge(gelu_done, 4 + unit * FC + fc + 1)
                    if fc < FC - 1:
                        pe.wait_ge(low_pool, (FC - 1) * (unit + 1) + fc + 1)
                    else:
                        pe.wait_ge(low_dve, 1 + unit + 1)
                    for j, (a, b) in enumerate(PASSES):
                        ins = mm(bank(4 + e % 2), w2[:, a, e, fc * P:(fc + 1) * P],
                                 hid_hl[:, b, (e % 2) * FC + fc, :], start=fc + j == 0, stop=fc == FC - 1 and j == 2)
                ins.then_inc(y2_mm, 1)

            def rows_again(g):
                pe.wait_ge(gated, 1 + g + 1)
                pe.wait_ge(out_ready, g + 1)
                for t in range(GT):
                    ins = nc.tensor.transpose(bank(7)[:, t * P:(t + 1) * P], acc_gb[:, t * P:(t + 1) * P], ident[:, :])
                ins.then_inc(outT_mm, 1)

            def experts(g, start=0):
                for e in range(start, E):
                    up(g, e)
                    down(g if e else g - 1, (e - 1) % E)
                    if e == 2 and not start:
                        rows_again(g - 1)

            up(0, 0)
            up(0, 1)
            down(0, 0)
            pe.wait_ge(w_ready, 1)
            for half in range(2):
                ins = nc.tensor.transpose(
                    bank(6)[:, half * P:(half + 1) * P],
                    w_exp[:, half * NT // 2:(half + 1) * NT // 2, :].rearrange("p t e -> p (t e)"), ident[:, :])
            ins.then_inc(w_rows_mm, 1)
            up(0, 2)
            down(0, 1)
            experts(0, start=3)
            with pe.Fori(1, NG) as g:
                experts(g)
            down(NG - 1, E - 1)
            rows_again(NG - 1)


_INS = ["L0_attn_x", "L0_attn_Wq", "L0_attn_bq", "L0_attn_Wk", "L0_attn_bk", "L0_attn_Wv", "L0_attn_bv",
        "L0_attn_Wo", "L0_attn_bo", "L0_ffn_W1", "L0_ffn_b1", "L0_ffn_W2", "L0_ffn_b2", "L0_ffn_gate_w",
        "L0_ffn_gate_b", "L0_ffn_temperature", "L0_c", "L0_wmod"]


def kernel(**inputs):
    import numpy as _np
    import concourse.bacc as _bacc
    from concourse import mybir as _mybir
    from concourse.bass_utils import run_bass_kernel_spmd as _run

    nc = _bacc.Bacc("TRN2", target_bir_lowering=False, num_devices=1)
    arrays, args = {}, []
    for name in _INS:
        a = _np.ascontiguousarray(inputs[name])
        if name == "L0_ffn_temperature":
            a = a.reshape(1)
        arrays[f"in_{name}"] = a
        args.append(nc.dram_tensor(f"in_{name}", a.shape, _mybir.dt.from_np(a.dtype), kind="ExternalInput").ap())
    shape = inputs["L0_attn_x"].shape
    out = nc.dram_tensor("out_0", shape, _mybir.dt.float32, kind="ExternalOutput").ap()
    adaln_block(nc, *args, out)
    r = _run(nc, [arrays], core_ids=[0])
    return r.results[0]["out_0"]
```
